# Optimizing a Trainium2 kernel written in Bass

```python
import numpy as np
import jax
import jax.numpy as jnp

def _softmax(x, axis=-1):
    return jax.nn.softmax(x, axis=axis)

def _gelu(x):
    return jax.nn.gelu(x, approximate=True)

def _silu(x):
    return jax.nn.silu(x)

def _sigmoid(x):
    return jax.nn.sigmoid(x)

def _layernorm(x, axis=-1, eps=1e-05):
    m = jnp.mean(x, axis=axis, keepdims=True)
    v = jnp.var(x, axis=axis, keepdims=True)
    return (x - m) / jnp.sqrt(v + eps)

def _scatter_add(tgt, idx, src, axis=0):
    return tgt.at[idx].add(src)

def _segment_sum(src, seg, n):
    return jax.ops.segment_sum(src, seg, n)
kernel_name = 'mk_sandwich_d1_jaxref_r4_5beb32'

def setup_inputs(seed: int=0):
    np.random.seed(seed)
    _w = jnp.asarray

    def _L0_attn_setup():
        import jax, jax.numpy as jnp
        import numpy as np
        B, S, D = (2, 512, 256)
        H, P = (16, 64)
        NUM_OUT = 256
        key = jax.random.key(seed)
        ks = jax.random.split(key, 9)
        sc = 0.05
        return {'x': jax.random.normal(ks[0], (B, S, D), jnp.float32), 'q_w': jax.random.normal(ks[1], (H, P, D), jnp.float32) * sc, 'q_b': jax.random.normal(ks[2], (H, 1, P), jnp.float32) * sc, 'k_w': jax.random.normal(ks[3], (H, P, D), jnp.float32) * sc, 'k_b': jax.random.normal(ks[4], (H, 1, P), jnp.float32) * sc, 'v_w': jax.random.normal(ks[5], (H, P, D), jnp.float32) * sc, 'v_b': jax.random.normal(ks[6], (H, 1, P), jnp.float32) * sc, 'l_w': jax.random.normal(ks[7], (NUM_OUT, P * H), jnp.float32) * sc, 'l_b': jax.random.normal(ks[8], (1, NUM_OUT), jnp.float32) * sc}
    _L0_attn_in = _L0_attn_setup()

    def _L0_ffn_setup():
        import jax, jax.numpy as jnp
        import numpy as np
        DIM = 256

        def _reference_tuple_inner(x, W_r, W_k, W_v, mu_r, mu_k):
            B, T, C = x.shape
            x_prev = jnp.concatenate([jnp.zeros((B, 1, C), x.dtype), x[:, :-1, :]], axis=1)
            xr = mu_r * x + (1.0 - mu_r) * x_prev
            xk = mu_k * x + (1.0 - mu_k) * x_prev
            r = jax.nn.sigmoid(jnp.einsum('btc,dc->btd', xr, W_r))
            k = jnp.einsum('btc,dc->btd', xk, W_k)
            k_act = jnp.square(jax.nn.relu(k))
            out = r * jnp.einsum('btc,dc->btd', k_act, W_v)
            new_state = x[:, -1, :]
            return (out, new_state)
        key = jax.random.key(seed)
        ks = jax.random.split(key, 6)
        B, T, C = (8, 512, DIM)
        x = jax.random.normal(ks[0], (B, T, C), dtype=jnp.float32)
        s = 1.0 / np.sqrt(C)
        W_r = jax.random.uniform(ks[1], (C, C), jnp.float32, -s, s)
        W_k = jax.random.uniform(ks[2], (C, C), jnp.float32, -s, s)
        W_v = jax.random.uniform(ks[3], (C, C), jnp.float32, -s, s)
        mu_r = jax.random.uniform(ks[4], (C,), jnp.float32)
        mu_k = jax.random.uniform(ks[5], (C,), jnp.float32)
        return {'x': x, 'W_r': W_r, 'W_k': W_k, 'W_v': W_v, 'mu_r': mu_r, 'mu_k': mu_k}
    _L0_ffn_in = _L0_ffn_setup()
    _d = {'L0_attn_x': _L0_attn_in['x'], 'L0_attn_q_w': _L0_attn_in['q_w'], 'L0_attn_q_b': _L0_attn_in['q_b'], 'L0_attn_k_w': _L0_attn_in['k_w'], 'L0_attn_k_b': _L0_attn_in['k_b'], 'L0_attn_v_w': _L0_attn_in['v_w'], 'L0_attn_v_b': _L0_attn_in['v_b'], 'L0_attn_l_w': _L0_attn_in['l_w'], 'L0_attn_l_b': _L0_attn_in['l_b'], 'L0_ffn_W_r': _L0_ffn_in['W_r'], 'L0_ffn_W_k': _L0_ffn_in['W_k'], 'L0_ffn_W_v': _L0_ffn_in['W_v'], 'L0_ffn_mu_r': _L0_ffn_in['mu_r'], 'L0_ffn_mu_k': _L0_ffn_in['mu_k']}
    _x0 = _d['L0_attn_x']
    _d['L0_attn_x'] = jax.random.normal(jax.random.fold_in(jax.random.key(seed), 1), (8, 1024, 256), dtype=_x0.dtype)
    del _x0
    return _d

def reference(L0_attn_x, L0_attn_q_w, L0_attn_q_b, L0_attn_k_w, L0_attn_k_b, L0_attn_v_w, L0_attn_v_b, L0_attn_l_w, L0_attn_l_b, L0_ffn_W_r, L0_ffn_W_k, L0_ffn_W_v, L0_ffn_mu_r, L0_ffn_mu_k):

    def _L0_attn_ref(x, q_w, q_b, k_w, k_b, v_w, v_b, l_w, l_b):
        import jax, jax.numpy as jnp
        import numpy as np
        B, S, D = (2, 512, 256)
        H, P = (16, 64)
        NUM_OUT = 256
        q = jnp.einsum('bsd,hpd->bhsp', x, q_w) + q_b
        k = jnp.einsum('bsd,hpd->bhsp', x, k_w) + k_b
        v = jnp.einsum('bsd,hpd->bhsp', x, v_w) + v_b
        scores = jnp.einsum('bhqp,bhkp->bhqk', q, k) / jnp.sqrt(jnp.float32(P))
        attn = jax.nn.softmax(scores, axis=2)
        ctx = jnp.einsum('bhqk,bhkp->bqhp', attn, v)
        concat = ctx.reshape(ctx.shape[0], ctx.shape[1], H * P)
        out = concat @ l_w.T + l_b
        return out

    def _L0_ffn_ref(x, W_r, W_k, W_v, mu_r, mu_k):
        import jax, jax.numpy as jnp
        import numpy as np
        DIM = 256

        def _reference_tuple_inner(x, W_r, W_k, W_v, mu_r, mu_k):
            B, T, C = x.shape
            x_prev = jnp.concatenate([jnp.zeros((B, 1, C), x.dtype), x[:, :-1, :]], axis=1)
            xr = mu_r * x + (1.0 - mu_r) * x_prev
            xk = mu_k * x + (1.0 - mu_k) * x_prev
            r = jax.nn.sigmoid(jnp.einsum('btc,dc->btd', xr, W_r))
            k = jnp.einsum('btc,dc->btd', xk, W_k)
            k_act = jnp.square(jax.nn.relu(k))
            out = r * jnp.einsum('btc,dc->btd', k_act, W_v)
            new_state = x[:, -1, :]
            return (out, new_state)
        return _reference_tuple_inner(x, W_r, W_k, W_v, mu_r, mu_k)[0]
    x = L0_attn_x
    x = x + _layernorm(_L0_attn_ref(_layernorm(x, axis=-1), L0_attn_q_w, L0_attn_q_b, L0_attn_k_w, L0_attn_k_b, L0_attn_v_w, L0_attn_v_b, L0_attn_l_w, L0_attn_l_b), axis=-1)
    x = x + _layernorm(_L0_ffn_ref(_layernorm(x, axis=-1), L0_ffn_W_r, L0_ffn_W_k, L0_ffn_W_v, L0_ffn_mu_r, L0_ffn_mu_k), axis=-1)
    return x

_drawn_inputs = setup_inputs


def setup_inputs(seed=0):
    import zlib

    import numpy as np

    out = dict(_drawn_inputs(seed))
    spreads = {}
    factors = {}
    for name, (base, spread) in spreads.items():
        noise = np.random.default_rng([zlib.crc32(name.encode()), seed]).standard_normal(out[name].shape)
        drawn = base * np.exp(spread * noise) if base else spread * noise
        out[name] = jnp.asarray(drawn.astype(out[name].dtype))
    for name, factor in factors.items():
        out[name] = (out[name] * factor).astype(out[name].dtype)
    return out
```

```python
from contextlib import ExitStack

import concourse.bass as bass
from concourse import mybir

F32 = mybir.dt.float32
F32R = mybir.dt.float32r
ALU = mybir.AluOpType
ACT = mybir.ActivationFunctionType
AX = mybir.AxisListType

P = 128
HALF = 512
EPS = 1e-5


def attention_ffn_block(nc, x, wqk, bqk, wv, vb, wl, lb, ffn, mu, out, v_scr, c_scr):
    tokens, D = x.shape
    PAIRS = wqk.shape[0] - 1
    HP = PAIRS * P
    Dh = P // 2
    S = 1024
    B = tokens // S
    KT = S // P
    DC = D // P
    SLOTS = B * PAIRS
    assert PAIRS == 8 and KT == 8 and DC == 2 and S == 2 * HALF and B >= 3

    x_tiles = x.rearrange("(n p) d -> n p d", p=P)
    v_scr_slots = v_scr.rearrange("b g p k c -> (b g) p k c")
    c_scr_tiles = c_scr.rearrange("b t r g c -> (b t) r g c")
    out_tiles = out.rearrange("(n p) d -> n p d", p=P)

    with ExitStack() as ctx:
        def sb(name, shape, dt=F32):
            return ctx.enter_context(nc.sbuf_tensor(name, shape, dt))

        def sem(name):
            return ctx.enter_context(nc.semaphore(name))

        wv_hi, wv_lo = sb("wv_hi", [P, DC, HP], F32R), sb("wv_lo", [P, DC, HP], F32R)
        wl_hi, wl_lo = sb("wl_hi", [P, PAIRS, D], F32R), sb("wl_lo", [P, PAIRS, D], F32R)
        ffn_hi, ffn_lo = sb("ffn_hi", [P, 3, DC, D], F32R), sb("ffn_lo", [P, 3, DC, D], F32R)
        xt_hi, xt_lo = sb("xt_hi", [P, 2, DC, S], F32R), sb("xt_lo", [P, 2, DC, S], F32R)
        q_st = sb("q_st", [P, 2, 2, S], F32R)
        k_st = sb("k_st", [P, 2, 2, S], F32R)
        k_sw = sb("k_sw", [P, 2, 2, S], F32R)
        e_ring = sb("e_ring", [P, 4, S])
        qk_f = sb("qk_f", [P, 2, HALF])
        q_lo = sb("q_lo", [P, S], F32R)
        v_pair = sb("v_pair", [P, 2, KT, P])
        v_scaled = sb("v_scaled", [P, 2, P])
        v_out = sb("v_out", [P, HP])
        v_bias = sb("v_bias", [P, HP])
        c_out = sb("c_out", [P, S])
        c_in = sb("c_in", [P, PAIRS, P])
        c_hi, c_lo = sb("c_hi", [P, PAIRS, P], F32R), sb("c_lo", [P, PAIRS, P], F32R)
        w_raw = sb("w_raw", [P, DC, 2 * P])
        w_hi, w_lo = sb("w_hi", [P, DC, 2 * P], F32R), sb("w_lo", [P, DC, 2 * P], F32R)
        x_n = sb("x_n", [P, D])
        xn_hi, xn_lo = sb("xn_hi", [P, DC, P], F32R), sb("xn_lo", [P, DC, P], F32R)
        att = sb("att", [P, D])
        x1 = sb("x1", [P, 2, D])
        y_t = sb("y_t", [P, DC, P + 1])
        mix = sb("mix", [P, 2, DC, P])
        mix_hi, mix_lo = sb("mix_hi", [P, 2, DC, P], F32R), sb("mix_lo", [P, 2, DC, P], F32R)
        k_sq = sb("k_sq", [P, DC, P])
        ka_hi, ka_lo = sb("ka_hi", [P, DC, P], F32R), sb("ka_lo", [P, DC, P], F32R)
        gate, ff = sb("gate", [P, D]), sb("ff", [P, D])
        l_bias = sb("l_bias", [P, D])
        ident = sb("ident", [P, P])
        qk_bias = sb("qk_bias", [P, 2, PAIRS + 1])
        mu_sb = sb("mu_sb", [P, 2, DC])
        not_first = sb("not_first", [P, KT])
        neg_half = sb("neg_half", [P, 1])
        neg_max = sb("neg_max", [P, 2, 2])
        e_sum, e_inv = sb("e_sum", [P, 2, 2]), sb("e_inv", [P, 2, 2])
        stats = sb("stats", [P, 4, 6])
        mean_var = sb("mean_var", [P, 4, 2])
        var_eps, rstd = sb("var_eps", [P, 4]), sb("rstd", [P, 4])
        LN_IN, LN_ATT, LN_X1, LN_FF = range(4)

        score = [ctx.enter_context(nc.psum_tensor(f"score{h}", [P, S], F32)) for h in range(2)]
        context = ctx.enter_context(nc.psum_tensor("context", [P, S], F32))
        side = [ctx.enter_context(nc.psum_tensor(f"side{j}", [P, HALF], F32)) for j in range(2)]

        def sems(names):
            return [sem(n) for n in names.split()]

        bias_dma, wv_dma, wl_dma, ffn_dma, pool_ready, wv_split, weights_split, bias_ready = sems(
            "bias_dma wv_dma wl_dma ffn_dma pool_ready wv_split weights_split bias_ready")
        scores_done, context_done, xn_transposed, v_done, qk_done = sems(
            "scores_done context_done xn_transposed v_done qk_done")
        att_done, y_transposed, ffk_done, ffr_done, ffv_done = sems(
            "att_done y_transposed ffk_done ffr_done ffv_done")
        max_done, inv_done, in_step, hi_done, c_out_dve, post_step, tail_step = sems(
            "max_done inv_done in_step hi_done c_out_dve post_step tail_step")
        exp_done, f_done, k1_hi_done, w_hi_done, xt_done, y_step, ff_step, c_out_act = sems(
            "exp_done f_done k1_hi_done w_hi_done xt_done y_step ff_step c_out_act")
        v_scaled_done, lo_first, lo_done, w_lo_done, c_lo_done, ka_lo_done = sems(
            "v_scaled_done lo_first lo_done w_lo_done c_lo_done ka_lo_done")
        rstd_in, rstd_att, rstd_x1, rstd_ff = sems("rstd_in rstd_att rstd_x1 rstd_ff")
        x_in_dma, w_raw_dma, x_res_dma, c_in_dma, v_pair_dma, v_out_dma, q_dma = sems(
            "x_in_dma w_raw_dma x_res_dma c_in_dma v_pair_dma v_out_dma q_dma")
        k_dma = sems("k_dma0 k_dma1")
        c_out_dma, out_dma = sems("c_out_dma out_dma")

        IN_STEPS, POST_STEPS, TAIL_STEPS, Y_STEPS, FF_STEPS = 8, 15, 10, 2, 2
        AHEAD = {
            "pe": ((context_done, 2), (xn_transposed, 1), (v_done, 2), (qk_done, 4), (att_done, 1),
                   (y_transposed, 1), (ffr_done, 1), (ffv_done, 1)),
            "dve": ((in_step, IN_STEPS), (post_step, POST_STEPS), (tail_step, 2 * TAIL_STEPS), (c_out_dve, 1)),
            "act": ((exp_done, 2), (xt_done, 1), (c_out_act, 1)),
            "pool": ((v_scaled_done, 8), (lo_done, 2), (w_lo_done, 1), (c_lo_done, 1), (ka_lo_done, 1)),
            "sp": ((v_out_dma, 16), (q_dma, 32), (c_out_dma, 16), (out_dma, 16)),
        }

        sp_passed, pool_passed, act_passed, dve_passed = sems("sp_passed pool_passed act_passed dve_passed")

        def exp_at(i, kt, h):
            return i * 16 + (kt * 2 + h + 3)

        def context_at(i, kt):
            return i * 8 + (kt + 3)

        def in_at(m, step):
            return m * IN_STEPS + (step + IN_STEPS)

        def post_at(n, step):
            return n * POST_STEPS + (step + POST_STEPS)

        def tail_at(n, step):
            return n * TAIL_STEPS + (step + 2 * TAIL_STEPS)

        def y_at(n, step):
            return n * Y_STEPS + step

        def ff_at(n, step):
            return n * FF_STEPS + step

        def f_at(n, u):
            return n * 4 + (u + 1)

        def lo_at(n, u):
            return n * 4 + (u + 3)

        def qk_at(n, u):
            return n * 4 + (u + 5)

        def v_at(m, c):
            return m * 2 + (c + 3)

        class Slot:

            def __init__(self, i, b, p, par, qk=True, pre=True, post=True, tail=True, more=True):
                self.i, self.b, self.p, self.par, self.more = i, b, p, par, more
                self.qk, self.pre, self.post, self.tail = qk, pre, post, tail

        def walk(fori, first_tiles, slot, last_tiles):
            first_tiles()
            with fori(0, 4) as q:
                for par in range(2):
                    slot(Slot(q * 2 + par, 0, q * 2 + par, par, post=False, tail=False))
            slot(Slot(8, 1, 0, 0, tail=False))
            slot(Slot(9, 1, 1, 1))
            with fori(0, 3) as q:
                for par in range(2):
                    slot(Slot(q * 2 + (10 + par), 1, q * 2 + (2 + par), par))
            with fori(2, B - 1) as b:
                with fori(0, 4) as q:
                    for par in range(2):
                        slot(Slot(b * 8 + q * 2 + par, b, q * 2 + par, par))
            first = SLOTS - 8
            with fori(0, 3) as q:
                for par in range(2):
                    slot(Slot(q * 2 + (first + par), B - 1, q * 2 + par, par, pre=False))
            slot(Slot(first + 6, B - 1, 6, 0, pre=False))
            slot(Slot(first + 7, B - 1, 7, 1, pre=False, qk=False, more=False))
            last_tiles()

        def halves(c):
            return slice(c * HALF, (c + 1) * HALF)

        def head_rows(h):
            return slice(h * Dh, (h + 1) * Dh)

        block = ctx.enter_context(nc.Block())

        @block.sync
        def _(sp):
            for s, n in AHEAD["sp"]:
                sp.sem_inc(s, n)
            sp.dma_start(e_ring[:, 0:2, :], wv).then_inc(wv_dma, 16)
            sp.dma_start(v_bias[:, :], vb.partition_broadcast(P)).then_inc(bias_dma, 16)
            sp.dma_start(qk_bias[:, :, :], bqk).then_inc(bias_dma, 16)
            sp.dma_start(l_bias[:, :], lb.partition_broadcast(P)).then_inc(bias_dma, 16)
            sp.dma_start(mu_sb[:, :, :], mu).then_inc(bias_dma, 16)

            def load_x(m):
                sp.wait_ge(xn_transposed, m + 1)
                sp.sem_inc(sp_passed, 1)
                sp.dma_start(x_n[:, :], x_tiles[m]).then_inc(x_in_dma, 16)

            def load_w(n, pair):
                sp.wait_ge(w_lo_done, n + 1)
                sp.sem_inc(sp_passed, 1)
                sp.dma_start(w_raw[:, :, :], wqk[pair]).then_inc(w_raw_dma, 16)

            def store_v(m, b, t):
                sp.wait_ge(in_step, in_at(m, 8))
                sp.sem_inc(sp_passed, 1)
                sp.dma_start(v_scr[b, :, :, t, :].rearrange("g p c -> p g c"),
                             v_out[:, :].rearrange("p (g c) -> p g c", c=P)).then_inc(v_out_dma, 16)

            def load_v(i, par):
                sp.wait_ge(v_scaled_done, i * 8)
                sp.sem_inc(sp_passed, 1)
                sp.dma_start(v_pair[:, par, :, :], v_scr_slots[i]).then_inc(v_pair_dma, 16)

            def move_q(n, par):
                sp.wait_ge(lo_done, lo_at(n, 1))
                sp.sem_inc(sp_passed, 1)
                sp.dma_start(q_st[Dh:P, par, 0, :].bitcast(F32), q_lo[0:Dh, :].bitcast(F32)).then_inc(q_dma, 16)
                sp.dma_start(q_st[0:Dh, par, 1, :].bitcast(F32), q_lo[Dh:P, :].bitcast(F32)).then_inc(q_dma, 16)

            def move_k(n, par, c):
                sp.wait_ge(lo_done, lo_at(n, 2 + c))
                sp.sem_inc(sp_passed, 1)
                for dst, src in ((k_st, k_sw), (k_sw, k_st)):
                    sp.dma_start(dst[Dh:P, par, 0, halves(c)].bitcast(F32),
                                 src[0:Dh, par, 0, halves(c)].bitcast(F32)).then_inc(k_dma[c], 16)
                    sp.dma_start(dst[0:Dh, par, 1, halves(c)].bitcast(F32),
                                 src[Dh:P, par, 1, halves(c)].bitcast(F32)).then_inc(k_dma[c], 16)

            def load_post(n, par, stored):
                sp.wait_ge(tail_step, tail_at(n - 2, 10))
                sp.sem_inc(sp_passed, 1)
                sp.dma_start(x1[:, par, :], x_tiles[n]).then_inc(x_res_dma, 16)
                sp.wait_ge(c_lo_done, n + 1)
                sp.sem_inc(sp_passed, 1)
                sp.wait_ge(c_out_dma, stored)
                sp.sem_inc(sp_passed, 1)
                sp.dma_start(c_in[:, :, :], c_scr_tiles[n]).then_inc(c_in_dma, 16)

            def first_tiles():
                with sp.Fori(0, KT) as t:
                    load_x(t)
                    store_v(t, 0, t)
                sp.dma_start(c_out[:, :], ffn[:, 0:2, :]).then_inc(ffn_dma, 16)
                sp.dma_start(x1[:, :, :], ffn[:, 2, :]).then_inc(ffn_dma, 16)
                sp.dma_start(e_ring[:, 2:4, :], wl).then_inc(wl_dma, 16)
                load_w(0, 0)
                sp.wait_ge(v_out_dma, 16 * (KT + 1))
                load_v(0, 0)
                move_q(0, 0)
                move_k(0, 0, 0)
                move_k(0, 0, 1)

            def slot(s):
                if s.pre:
                    load_x(s.i + 8)
                if s.qk:
                    load_w(s.i + 1, s.p + 1)
                if s.post:
                    load_post(s.i - 8, s.par, s.b * 128 + 16)
                if s.pre:
                    store_v(s.i + 8, s.b + 1, s.p)
                    sp.wait_ge(v_out_dma, (s.i + 8) * 16 + 32)
                    sp.sem_inc(sp_passed, 1)
                if s.more:
                    load_v(s.i + 1, 1 - s.par)
                if s.qk:
                    move_q(s.i + 1, 1 - s.par)
                    move_k(s.i + 1, 1 - s.par, 0)
                    move_k(s.i + 1, 1 - s.par, 1)

            def last_tiles():
                with sp.Fori(0, KT // 2) as q:
                    for par in range(2):
                        load_post(q * 2 + (SLOTS - 8 + par), par, 16 * SLOTS + 16)

            walk(sp.Fori, first_tiles, slot, last_tiles)
            sp.wait_ge(out_dma, 16 * (SLOTS + 1))
            sp.wait_ge(v_out_dma, 16 * (SLOTS + 1))
            sp.wait_ge(c_out_dma, 16 * (SLOTS + 1))

        @block.gpsimd
        def _(pool):
            for s, n in AHEAD["pool"]:
                pool.sem_inc(s, n)
            pool.memset(neg_half[:, :], -0.5)
            pool.memset(not_first[:, :], 1.0)
            pool.memset(ident[:, :], 0.0).then_inc(pool_ready, 1)
            pool.wait_ge(pool_ready, 1)
            pool.affine_select(out=ident[:, :], in_=ident[:, :], compare_op=ALU.not_equal, fill=1.0, base=0,
                               pattern=[[-1, P]], channel_multiplier=1)
            pool.memset(not_first[:, 0:1], 0.0).then_inc(pool_ready, 1)
            pool.wait_ge(pool_ready, 2)

            def low(out, full, high):
                return pool.tensor_tensor(out, full, high.bitcast(F32), ALU.subtract)

            def power(row, at, step, done):
                pool.wait_ge(at, step)
                pool.sem_inc(pool_passed, 1)
                pool.tensor_tensor(rstd[:, row:row + 1], var_eps[:, row:row + 1], neg_half[:, :],
                                   ALU.pow).then_inc(done, 1)

            def split_w(n):
                pool.wait_ge(w_hi_done, n + 1)
                pool.sem_inc(pool_passed, 1)
                pool.wait_ge(qk_done, qk_at(n - 1, 3))
                pool.sem_inc(pool_passed, 1)
                low(w_lo[:, :, :], w_raw[:, :, :], w_hi[:, :, :]).then_inc(w_lo_done, 1)

            def split_qk(n, par, u):
                if u < 3:
                    pool.wait_ge(hi_done, n * 3 + (u + 1))
                else:
                    pool.wait_ge(k1_hi_done, n + 1)
                pool.sem_inc(pool_passed, 1)
                if u == 0:
                    pool.wait_ge(q_dma, n * 32 + 32)
                    pool.sem_inc(pool_passed, 1)
                for h, done in enumerate((lo_first, lo_done)):
                    rows = head_rows(h)
                    if u < 2:
                        low(q_lo[rows, halves(u)], qk_f[rows, u, :],
                            q_st[rows, par, h, halves(u)]).then_inc(done, 1)
                    else:
                        low(k_sw[rows, par, h, halves(u - 2)], qk_f[rows, u - 2, :],
                            k_st[rows, par, h, halves(u - 2)]).then_inc(done, 1)
                    pool.wait_ge(done, n * 4 + (u + 1) if h == 0 else lo_at(n, u))
                    pool.sem_inc(pool_passed, 1)

            def scale_v(s, kt):
                pool.wait_ge(inv_done, s.i * 8 + (kt + 1))
                pool.sem_inc(pool_passed, 1)
                if kt == 0:
                    pool.wait_ge(v_pair_dma, s.i * 16 + 16)
                    pool.sem_inc(pool_passed, 1)
                pool.tensor_tensor(v_scaled[:, kt % 2, :].rearrange("p (h c) -> p h c", h=2),
                                   v_pair[:, s.par, kt, :].rearrange("p (h c) -> p h c", h=2),
                                   e_inv[:, kt % 2, :].unsqueeze(2).broadcast_to([P, 2, Dh]),
                                   ALU.mult).then_inc(v_scaled_done, 1)

            def split_context(n):
                pool.wait_ge(post_step, post_at(n, 1))
                pool.sem_inc(pool_passed, 1)
                pool.wait_ge(att_done, n + 1)
                pool.sem_inc(pool_passed, 1)
                low(c_lo[:, :, :], c_in[:, :, :], c_hi[:, :, :]).then_inc(c_lo_done, 1)

            def split_ka(n):
                pool.wait_ge(tail_step, tail_at(n, 2))
                pool.sem_inc(pool_passed, 1)
                low(ka_lo[:, :, :], k_sq[:, :, :], ka_hi[:, :, :]).then_inc(ka_lo_done, 1)

            def first_tiles():
                with pool.Fori(0, KT) as t:
                    power(LN_IN, in_step, in_at(t, 3), rstd_in)
                split_w(0)
                for u in range(4):
                    split_qk(0, 0, u)

            def slot(s):
                for kt in range(KT):
                    scale_v(s, kt)
                    if kt == 0 and s.pre:
                        power(LN_IN, in_step, in_at(s.i + 8, 3), rstd_in)
                    if kt == 0 and s.qk:
                        split_w(s.i + 1)
                    if kt == 1 and s.tail:
                        split_ka(s.i - 9)
                    if kt == 2 and s.post:
                        split_context(s.i - 8)
                    if kt == 5 and s.post:
                        power(LN_ATT, post_step, post_at(s.i - 8, 5), rstd_att)
                    if 3 <= kt <= 6 and s.qk:
                        split_qk(s.i + 1, 1 - s.par, kt - 3)
                    if kt == 5 and s.post:
                        power(LN_X1, post_step, post_at(s.i - 8, 10), rstd_x1)
                    if kt == 6 and s.tail:
                        power(LN_FF, tail_step, tail_at(s.i - 9, 8), rstd_ff)

            def last_tiles():
                split_ka(SLOTS - 9)
                power(LN_FF, tail_step, tail_at(SLOTS - 9, 8), rstd_ff)
                with pool.Fori(SLOTS - 8, SLOTS) as n:
                    split_context(n)
                    power(LN_ATT, post_step, post_at(n, 5), rstd_att)
                    power(LN_X1, post_step, post_at(n, 10), rstd_x1)
                    split_ka(n)
                    power(LN_FF, tail_step, tail_at(n, 8), rstd_ff)

            walk(pool.Fori, first_tiles, slot, last_tiles)

        @block.scalar
        def _(act):
            for s, n in AHEAD["act"]:
                act.sem_inc(s, n)
            act.wait_ge(bias_dma, 64)
            act.activation(qk_bias[:, 0, :], qk_bias[:, 0, :], ACT.Copy, scale=Dh ** -0.5).then_inc(bias_ready, 1)
            act.wait_ge(bias_ready, 1)

            def high_w(n):
                act.wait_ge(w_raw_dma, n * 16 + 16)
                act.wait_ge(qk_done, qk_at(n - 1, 3))
                act.activation(w_hi[:, :, :], w_raw[:, :, :], ACT.Copy).then_inc(w_hi_done, 1)

            def keep_xt(m, buf, t):
                act.wait_ge(in_step, in_at(m, 6))
                act.sem_inc(act_passed, 1)
                for dst, src in ((xt_hi, xn_hi), (xt_lo, xn_lo)):
                    last = act.activation(dst[:, buf, :, bass.ts(t, P)], src[:, :, :].bitcast(F32), ACT.Copy)
                last.then_inc(xt_done, 1)

            def full_qk(n, pair, u):
                act.wait_ge(qk_done, qk_at(n, u))
                act.wait_ge(lo_done, lo_at(n, u - 2))
                act.sem_inc(act_passed, 1)
                act.activation(qk_f[:, u % 2, :], side[1][:, :], ACT.Identity,
                               bias=qk_bias[:, u // 2, bass.ds(pair, 1)],
                               scale=Dh ** -0.5 if u < 2 else 1.0).then_inc(f_done, 1)

            def high_k1(n, par):
                act.wait_ge(f_done, f_at(n, 3))
                for h in range(2):
                    last = act.activation(k_st[head_rows(h), par, h, halves(1)], qk_f[head_rows(h), 1, :], ACT.Copy)
                last.then_inc(k1_hi_done, 1)

            def exps(i, kt):
                for h in range(2):
                    act.wait_ge(max_done, i * 16 + (kt * 2 + h + 1))
                    act.wait_ge(context_done, i * 8 + (kt + 1))
                    act.activation(e_ring[:, (2 * kt + h) % 4, :], score[h][:, :], ACT.Exp,
                                   bias=neg_max[:, kt % 2, h:h + 1],
                                   accum_out=e_sum[:, kt % 2, h:h + 1]).then_inc(exp_done, 1)

            def ff_relu(n):
                act.wait_ge(ffk_done, n + 1)
                act.wait_ge(ka_lo_done, n + 1)
                act.activation(k_sq[:, :, :], side[1][:, 0:D].rearrange("p (c t) -> p c t", c=DC),
                               ACT.Relu).then_inc(ff_step, 1)

            def ff_gate(n):
                act.wait_ge(ffr_done, n + 2)
                act.wait_ge(tail_step, tail_at(n - 1, 5))
                act.activation(gate[:, :], side[0][:, 0:D], ACT.Exp, scale=-1.0).then_inc(ff_step, 1)

            def keep_y(n, t):
                act.wait_ge(post_step, post_at(n - 1, 13))
                act.sem_inc(act_passed, 1)
                act.activation(y_t[:, :, 0:1], y_t[:, :, P:P + 1], ACT.Copy,
                               scale=not_first[:, bass.ds(t, 1)]).then_inc(y_step, 1)
                act.wait_ge(y_transposed, n + 2)
                act.wait_ge(y_step, y_at(n, 1))
                act.activation(y_t[:, :, 1:P + 1], side[1][:, 0:D].rearrange("p (c t) -> p c t", c=DC),
                               ACT.Copy).then_inc(y_step, 1)

            def keep_context(i):
                act.wait_ge(context_done, context_at(i, 7))
                act.wait_ge(c_out_dma, i * 16 + 16)
                act.activation(c_out[:, halves(0)], context[:, halves(0)], ACT.Copy).then_inc(c_out_act, 1)

            def store_context(i, b, p):
                act.wait_ge(c_out_act, i + 2)
                act.wait_ge(c_out_dve, i + 2)
                act.dma_start(c_scr[b, :, :, p, :].rearrange("t r c -> r t c"),
                              c_out[:, :].rearrange("r (t c) -> r t c", c=P)).then_inc(c_out_dma, 16)

            def store_out(n):
                act.wait_ge(tail_step, tail_at(n, 10))
                act.dma_start(out_tiles[n], ff[:, :]).then_inc(out_dma, 16)

            def first_tiles():
                with act.Fori(0, KT) as t:
                    keep_xt(t, 0, t)
                high_w(0)
                for u in range(4):
                    full_qk(0, 0, u)
                high_k1(0, 0)
                act.wait_ge(weights_split, 1)
                act.sem_inc(act_passed, 1)
                exps(0, 0)

            def slot(s):
                for kt in range(KT):
                    if kt == 0 and s.qk:
                        high_w(s.i + 1)
                    if kt == 1 and s.tail:
                        ff_relu(s.i - 9)
                    if kt == 2 and s.tail:
                        ff_gate(s.i - 9)
                    if kt == 2 and s.pre:
                        keep_xt(s.i + 8, (s.b + 1) % 2, s.p)
                    if 3 <= kt <= 6 and s.qk:
                        full_qk(s.i + 1, s.p + 1, kt - 3)
                    if kt == 6 and s.qk:
                        high_k1(s.i + 1, 1 - s.par)
                    if kt == 7 and s.post:
                        keep_y(s.i - 8, s.p)
                    if kt < KT - 1:
                        exps(s.i, kt + 1)
                    elif s.more:
                        exps(s.i + 1, 0)
                keep_context(s.i)
                store_context(s.i, s.b, s.p)
                if s.tail:
                    store_out(s.i - 9)

            def last_tiles():
                def tail(n):
                    ff_relu(n)
                    ff_gate(n)
                    store_out(n)

                tail(SLOTS - 9)
                with act.Fori(0, KT) as t:
                    keep_y(t + (SLOTS - 8), t)
                    tail(t + (SLOTS - 8))

            walk(act.Fori, first_tiles, slot, last_tiles)

        @block.vector
        def _(dve):
            for s, n in AHEAD["dve"]:
                dve.sem_inc(s, n)
            dve.memset(y_t[:, :, :], 0.0)

            def high(out, full):
                return dve.tensor_copy(out, full)

            def low(out, full, high_part):
                return dve.tensor_tensor(out, full, high_part.bitcast(F32), ALU.subtract)

            def moments(row, src, sem_, at):
                dve.wait_ge(sem_, at(0))
                dve.bn_stats(stats[:, row, :], src).then_inc(sem_, 1)
                dve.wait_ge(sem_, at(1))
                dve.sem_inc(dve_passed, 1)
                dve.bn_aggr(mean_var[:, row, :], stats[:, row, :]).then_inc(sem_, 1)
                dve.wait_ge(sem_, at(2))
                dve.tensor_scalar(var_eps[:, row:row + 1], mean_var[:, row, 1:2], EPS, None,
                                  ALU.add).then_inc(sem_, 1)

            def normalise(out, src, row):
                return dve.tensor_scalar(out, src, mean_var[:, row, 0:1], rstd[:, row:row + 1],
                                         ALU.subtract, ALU.mult)

            def in_moments(m):
                dve.wait_ge(x_in_dma, m * 16 + 16)
                moments(LN_IN, x_n[:, :], in_step, lambda k: in_at(m, k))

            def in_norm(m):
                dve.wait_ge(rstd_in, m + 1)
                normalise(x_n[:, :], x_n[:, :], LN_IN).then_inc(in_step, 1)

            def in_split(m):
                dve.wait_ge(xn_transposed, m + 2)
                dve.wait_ge(v_done, v_at(m - 1, 1))
                dve.wait_ge(xt_done, m + 1)
                xn = side[0][:, 0:D].rearrange("p (c t) -> p c t", c=DC)
                high(xn_hi[:, :, :], xn).then_inc(in_step, 1)
                dve.wait_ge(in_step, in_at(m, 5))
                low(xn_lo[:, :, :], xn, xn_hi[:, :, :]).then_inc(in_step, 1)

            def in_v(m, c):
                dve.wait_ge(v_done, v_at(m, c))
                if c == 0:
                    dve.wait_ge(v_out_dma, m * 16 + 16)
                dve.tensor_tensor(v_out[:, halves(c)], side[1 - c][:, :], v_bias[:, halves(c)],
                                  ALU.add).then_inc(in_step, 1)

            def high_qk(n, par, u):
                dve.wait_ge(f_done, f_at(n, u))
                for h in range(2):
                    dst = q_st if u < 2 else k_st
                    last = high(dst[head_rows(h), par, h, halves(u % 2)], qk_f[head_rows(h), u % 2, :])
                last.then_inc(hi_done, 1)

            def maxima(i, kt):
                for h in range(2):
                    dve.wait_ge(scores_done, i * 16 + (kt * 2 + h + 1))
                    dve.reduce_max(neg_max[:, kt % 2, h:h + 1], score[h][:, :], AX.X,
                                   negate=True).then_inc(max_done, 1)

            def inverse(i, kt):
                dve.wait_ge(exp_done, exp_at(i, kt, 1))
                dve.reciprocal(e_inv[:, kt % 2, :], e_sum[:, kt % 2, :]).then_inc(inv_done, 1)

            def post_high_context(n):
                dve.wait_ge(c_in_dma, n * 16 + 16)
                dve.wait_ge(att_done, n + 1)
                high(c_hi[:, :, :], c_in[:, :, :]).then_inc(post_step, 1)

            def post_attention(n):
                dve.wait_ge(att_done, n + 2)
                dve.wait_ge(y_transposed, n + 1)
                dve.tensor_tensor(att[:, :], side[0][:, 0:D], l_bias[:, :], ALU.add).then_inc(post_step, 1)
                moments(LN_ATT, att[:, :], post_step, lambda k: post_at(n, 2 + k))

            def post_residual(n, par):
                dve.wait_ge(rstd_att, n + 1)
                normalise(att[:, :], att[:, :], LN_ATT).then_inc(post_step, 1)
                dve.wait_ge(x_res_dma, n * 16 + 16)
                dve.wait_ge(post_step, post_at(n, 6))
                dve.tensor_tensor(x1[:, par, :], att[:, :], x1[:, par, :], ALU.add).then_inc(post_step, 1)
                moments(LN_X1, x1[:, par, :], post_step, lambda k: post_at(n, 7 + k))

            def post_y(n, par):
                dve.wait_ge(rstd_x1, n + 1)
                normalise(att[:, :], x1[:, par, :], LN_X1).then_inc(post_step, 1)

            def post_mix(n):
                dve.wait_ge(y_step, y_at(n, 2))
                dve.tensor_tensor(mix[:, 1, :, :], y_t[:, :, 1:P + 1], y_t[:, :, 0:P],
                                  ALU.subtract).then_inc(post_step, 1)
                dve.wait_ge(post_step, post_at(n, 12))
                for w in range(2):
                    for c in range(DC):
                        last = dve.scalar_tensor_tensor(mix[:, w, c, :], mix[:, 1, c, :], mu_sb[:, w, c:c + 1],
                                                        y_t[:, c, 0:P], ALU.mult, ALU.add)
                last.then_inc(post_step, 1)
                dve.wait_ge(post_step, post_at(n, 13))
                dve.wait_ge(ffr_done, n + 1)
                high(mix_hi[:, :, :, :], mix[:, :, :, :]).then_inc(post_step, 1)
                dve.wait_ge(post_step, post_at(n, 14))
                low(mix_lo[:, :, :, :], mix[:, :, :, :], mix_hi[:, :, :, :]).then_inc(post_step, 1)

            def tail_square(n):
                dve.wait_ge(ff_step, ff_at(n, 1))
                dve.tensor_tensor(k_sq[:, :, :], k_sq[:, :, :], k_sq[:, :, :], ALU.mult).then_inc(tail_step, 1)
                dve.wait_ge(tail_step, tail_at(n, 1))
                dve.wait_ge(ffv_done, n + 1)
                high(ka_hi[:, :, :], k_sq[:, :, :]).then_inc(tail_step, 1)

            def tail_gate(n):
                dve.wait_ge(ff_step, ff_at(n, 2))
                dve.tensor_scalar(gate[:, :], gate[:, :], 1.0, None, ALU.add).then_inc(tail_step, 1)
                dve.wait_ge(tail_step, tail_at(n, 3))
                dve.reciprocal(gate[:, :], gate[:, :]).then_inc(tail_step, 1)

            def tail_product(n):
                dve.wait_ge(ffv_done, n + 2)
                dve.wait_ge(out_dma, n * 16 + 16)
                dve.wait_ge(tail_step, tail_at(n, 4))
                dve.tensor_tensor(ff[:, :], side[0][:, 0:D], gate[:, :], ALU.mult).then_inc(tail_step, 1)
                moments(LN_FF, ff[:, :], tail_step, lambda k: tail_at(n, 5 + k))

            def tail_out(n, par):
                dve.wait_ge(rstd_ff, n + 1)
                normalise(ff[:, :], ff[:, :], LN_FF).then_inc(tail_step, 1)
                dve.wait_ge(tail_step, tail_at(n, 9))
                dve.tensor_tensor(ff[:, :], ff[:, :], x1[:, par, :], ALU.add).then_inc(tail_step, 1)

            def keep_context(i):
                dve.wait_ge(context_done, context_at(i, 7))
                dve.wait_ge(c_out_dma, i * 16 + 16)
                dve.tensor_copy(c_out[:, halves(1)], context[:, halves(1)]).then_inc(c_out_dve, 1)

            def first_tiles():
                dve.wait_ge(bias_dma, 64)
                dve.wait_ge(wv_dma, 16)
                raw = e_ring[:, 0:2, :]
                high(wv_hi[:, :, :], raw).then_inc(wv_split, 1)
                dve.wait_ge(wv_split, 1)
                low(wv_lo[:, :, :], raw, wv_hi[:, :, :]).then_inc(wv_split, 1)
                with dve.Fori(0, KT) as t:
                    in_moments(t)
                    in_norm(t)
                    in_split(t)
                    in_v(t, 0)
                    in_v(t, 1)
                dve.wait_ge(wl_dma, 16)
                raw_l = e_ring[:, 2:4, :].rearrange("p a c -> p (a c)").rearrange("p (g d) -> p g d", d=D)
                raw_rk = c_out[:, :].rearrange("p (w c d) -> p w c d", w=2, c=DC)
                high(wl_hi[:, :, :], raw_l)
                dve.wait_ge(ffn_dma, 32)
                high(ffn_hi[:, 0:2, :, :], raw_rk)
                high(ffn_hi[:, 2, :, :], x1[:, :, :]).then_inc(wv_split, 1)
                dve.wait_ge(wv_split, 3)
                low(wl_lo[:, :, :], raw_l, wl_hi[:, :, :])
                low(ffn_lo[:, 0:2, :, :], raw_rk, ffn_hi[:, 0:2, :, :])
                low(ffn_lo[:, 2, :, :], x1[:, :, :], ffn_hi[:, 2, :, :]).then_inc(weights_split, 1)
                for u in range(3):
                    high_qk(0, 0, u)
                maxima(0, 0)

            def slot(s):
                m, n, o = s.i + 8, s.i - 8, s.i - 9
                for kt in range(KT):
                    inverse(s.i, kt)
                    if kt == 0 and s.pre:
                        in_moments(m)
                    if kt == 1 and s.pre:
                        in_split(m)
                    if kt == 2 and s.pre:
                        in_v(m, 0)
                    if kt == 3 and s.pre:
                        in_v(m, 1)
                    if kt == 5 and s.post:
                        post_attention(n)
                    if kt == 5 and s.qk:
                        high_qk(s.i + 1, 1 - s.par, 2)
                    if kt == 6 and s.post:
                        post_y(n, s.par)
                    if kt == 7 and s.tail:
                        tail_out(o, 1 - s.par)
                    if kt < KT - 1:
                        maxima(s.i, kt + 1)
                    elif s.more:
                        maxima(s.i + 1, 0)
                    if kt == 0 and s.pre:
                        in_norm(m)
                    if kt == 1 and s.tail:
                        tail_square(o)
                    if kt == 2 and s.post:
                        post_high_context(n)
                    if kt == 2 and s.tail:
                        tail_gate(o)
                    if 3 <= kt <= 4 and s.qk:
                        high_qk(s.i + 1, 1 - s.par, kt - 3)
                    if kt == 5 and s.post:
                        post_residual(n, s.par)
                    if kt == 6 and s.tail:
                        tail_product(o)
                    if kt == 7 and s.post:
                        post_mix(n)
                keep_context(s.i)

            def last_tiles():
                def tail(n, par):
                    tail_square(n)
                    tail_gate(n)
                    tail_product(n)
                    tail_out(n, par)

                tail(SLOTS - 9, 1)
                with dve.Fori(0, KT // 2) as q:
                    for par in range(2):
                        n = q * 2 + (SLOTS - 8 + par)
                        post_high_context(n)
                        post_attention(n)
                        post_residual(n, par)
                        post_y(n, par)
                        post_mix(n)
                        tail(n, par)

            walk(dve.Fori, first_tiles, slot, last_tiles)

        @block.tensor
        def _(pe):
            for s, n in AHEAD["pe"]:
                pe.sem_inc(s, n)

            busy = [[], []]

            def take(bank, *freed):
                for s, at in busy[bank]:
                    pe.wait_ge(s, at)
                busy[bank] = list(freed)

            def split_product(out, pairs, first=True, last=True):
                terms = [t for a_hi, a_lo, b_hi, b_lo in pairs
                         for t in ((a_hi, b_hi), (a_hi, b_lo), (a_lo, b_hi))]
                for k, (a, b) in enumerate(terms):
                    mm = pe.matmul(out, a, b, start=first and k == 0, stop=last and k == len(terms) - 1)
                return mm

            def transpose_xn(m):
                take(0, (in_step, in_at(m, 6)))
                pe.wait_ge(in_step, in_at(m, 4))
                for c in range(DC):
                    mm = pe.transpose(side[0][:, bass.ts(c, P)], x_n[:, bass.ts(c, P)], ident[:, :])
                mm.then_inc(xn_transposed, 1)

            def project_v(m, c):
                take(1 - c, (in_step, in_at(m, 7 + c)))
                pe.wait_ge(in_step, in_at(m, 6))
                split_product(side[1 - c][:, :],
                              [(xn_hi[:, k, :], xn_lo[:, k, :], wv_hi[:, k, halves(c)], wv_lo[:, k, halves(c)])
                               for k in range(DC)]).then_inc(v_done, 1)

            def project_qk(n, u):
                take(1, (f_done, f_at(n, u)))
                if u == 0:
                    pe.wait_ge(w_lo_done, n + 2)
                    pe.wait_ge(xt_done, (n // 8) * 8 + 9)
                w = slice((u // 2) * P, (u // 2) * P + P)
                buf = (n // 8) % 2
                split_product(side[1][:, :],
                              [(w_hi[:, k, w], w_lo[:, k, w], xt_hi[:, buf, k, halves(u % 2)],
                                xt_lo[:, buf, k, halves(u % 2)]) for k in range(DC)]).then_inc(qk_done, 1)

            def scores(i, par, kt):
                if kt == 0:
                    pe.wait_ge(q_dma, i * 32 + 64)
                    pe.wait_ge(k_dma[0], i * 64 + 64)
                if kt == KT // 2:
                    pe.wait_ge(k_dma[1], i * 64 + 64)
                for h in range(2):
                    pe.wait_ge(exp_done, i * 16 + (kt * 2 + h + 1))
                    for c in range(2):
                        for k in (k_st, k_sw):
                            mm = pe.matmul(score[h][:, halves(c)], k[:, par, h, bass.ts(kt, P)],
                                           q_st[:, par, h, halves(c)], start=k is k_st, stop=k is k_sw)
                    mm.then_inc(scores_done, 1)

            def weighted(i, kt):
                if kt == 0:
                    pe.wait_ge(c_out_act, i + 1)
                    pe.wait_ge(c_out_dve, i + 1)
                pe.wait_ge(v_scaled_done, i * 8 + (kt + 9))
                for c in range(2):
                    for h in range(2):
                        mm = pe.matmul(context[head_rows(h), halves(c)], v_scaled[:, kt % 2, head_rows(h)],
                                       e_ring[:, (2 * kt + h) % 4, halves(c)], start=kt == 0, stop=kt == KT - 1)
                mm.then_inc(context_done, 1)

            def project_out(n, part):
                if part == 0:
                    take(0, (post_step, post_at(n, 2)))
                    pe.wait_ge(c_lo_done, n + 2)
                mm = split_product(side[0][:, 0:D],
                                   [(c_hi[:, g, :], c_lo[:, g, :], wl_hi[:, g, :], wl_lo[:, g, :])
                                    for g in range(part * PAIRS // 2, (part + 1) * PAIRS // 2)],
                                   first=part == 0, last=part == 1)
                if part == 1:
                    mm.then_inc(att_done, 1)

            def transpose_y(n):
                take(1, (y_step, y_at(n, 2)))
                pe.wait_ge(post_step, post_at(n, 11))
                for c in range(DC):
                    mm = pe.transpose(side[1][:, bass.ts(c, P)], att[:, bass.ts(c, P)], ident[:, :])
                mm.then_inc(y_transposed, 1)

            def feed_k(n):
                take(1, (ff_step, ff_at(n, 1)))
                pe.wait_ge(post_step, post_at(n, 15))
                for d in range(DC):
                    mm = split_product(side[1][:, bass.ts(d, P)],
                                       [(ffn_hi[:, 1, c, bass.ts(d, P)], ffn_lo[:, 1, c, bass.ts(d, P)],
                                         mix_hi[:, 1, c, :], mix_lo[:, 1, c, :]) for c in range(DC)])
                mm.then_inc(ffk_done, 1)

            def feed_r(n):
                take(0, (ff_step, ff_at(n, 2)))
                split_product(side[0][:, 0:D],
                              [(mix_hi[:, 0, c, :], mix_lo[:, 0, c, :], ffn_hi[:, 0, c, :], ffn_lo[:, 0, c, :])
                               for c in range(DC)]).then_inc(ffr_done, 1)

            def feed_v(n):
                take(0, (tail_step, tail_at(n, 5)))
                pe.wait_ge(ka_lo_done, n + 2)
                split_product(side[0][:, 0:D],
                              [(ka_hi[:, c, :], ka_lo[:, c, :], ffn_hi[:, 2, c, :], ffn_lo[:, 2, c, :])
                               for c in range(DC)]).then_inc(ffv_done, 1)

            def first_tiles():
                pe.wait_ge(pool_ready, 2)
                pe.wait_ge(wv_split, 2)
                with pe.Fori(0, KT) as t:
                    busy[:] = [[(in_step, in_at(t - 1, 8))], [(in_step, in_at(t - 1, 7))]]
                    transpose_xn(t)
                    project_v(t, 0)
                    project_v(t, 1)
                busy[:] = [[(in_step, in_at(KT - 1, 8))], [(in_step, in_at(KT - 1, 7))]]
                for u in range(4):
                    project_qk(0, u)
                pe.wait_ge(weights_split, 1)
                scores(0, 0, 0)

            def slot(s):
                m, n, o = s.i + 8, s.i - 8, s.i - 9
                busy[0] = ([(tail_step, tail_at(o - 1, 5)), (post_step, post_at(n - 1, 2))] if s.tail
                           else [(in_step, in_at(m - 1, 8))])
                busy[1] = [(y_step, y_at(n - 1, 2))] if s.tail else [(f_done, f_at(s.i, 3))]
                for kt in range(KT):
                    if kt < KT - 1:
                        scores(s.i, s.par, kt + 1)
                    elif s.more:
                        scores(s.i + 1, 1 - s.par, 0)
                    weighted(s.i, kt)
                    if kt == 0 and s.tail:
                        feed_k(o)
                    if kt == 0 and s.pre:
                        transpose_xn(m)
                    if kt == 1 and s.tail:
                        feed_r(o)
                    if kt == 1 and s.pre:
                        project_v(m, 0)
                    if kt == 2 and s.pre:
                        project_v(m, 1)
                    if 2 <= kt <= 3 and s.qk:
                        project_qk(s.i + 1, kt - 2)
                    if 3 <= kt <= 4 and s.post:
                        project_out(n, kt - 3)
                    if 4 <= kt <= 5 and s.qk:
                        project_qk(s.i + 1, kt - 2)
                    if kt == 5 and s.tail:
                        feed_v(o)
                    if kt == 6 and s.post:
                        transpose_y(n)

            def last_tiles():
                def tail(n):
                    feed_k(n)
                    feed_r(n)
                    feed_v(n)

                busy[:] = [[(tail_step, tail_at(SLOTS - 10, 5)), (post_step, post_at(SLOTS - 9, 2))],
                           [(y_step, y_at(SLOTS - 9, 2))]]
                tail(SLOTS - 9)
                with pe.Fori(SLOTS - 8, SLOTS) as n:
                    busy[:] = [[(tail_step, tail_at(n - 1, 5))], [(ff_step, ff_at(n - 1, 1))]]
                    project_out(n, 0)
                    project_out(n, 1)
                    transpose_y(n)
                    tail(n)

            walk(pe.Fori, first_tiles, slot, last_tiles)


def kernel(**inputs):
    import numpy as np
    import concourse.bacc as bacc
    from concourse.bass_utils import run_bass_kernel_spmd as run

    f = {k.replace("L0_", ""): np.asarray(v) for k, v in inputs.items()}
    x = f["attn_x"]
    B, S, D = x.shape
    H, Dh, _ = f["attn_q_w"].shape
    pairs, chunks = H * Dh // P, D // P

    def chunked(w):
        return w.T.reshape(chunks, P, -1).transpose(1, 0, 2)

    def by_pair(w):
        return chunked(w.reshape(H * Dh, D)).reshape(P, chunks, pairs, P).transpose(2, 0, 1, 3)

    wqk = np.concatenate([by_pair(f["attn_q_w"]), by_pair(f["attn_k_w"])], axis=-1)
    bqk = np.stack([f["attn_q_b"].reshape(pairs, P).T, f["attn_k_b"].reshape(pairs, P).T], axis=1)
    laid = {
        "x": x.reshape(B * S, D),
        "wqk": np.concatenate([wqk, wqk[:1]]),
        "bqk": np.concatenate([bqk, bqk[:, :, :1]], axis=-1),
        "wv": chunked(f["attn_v_w"].reshape(H * Dh, D)),
        "vb": f["attn_v_b"].reshape(H * Dh),
        "wl": f["attn_l_w"].T.reshape(pairs, P, D).transpose(1, 0, 2).reshape(P, 2, -1),
        "lb": f["attn_l_b"].reshape(D),
        "ffn": np.stack([chunked(f[f"ffn_W_{n}"]).reshape(P, -1) for n in "rkv"], axis=1),
        "mu": np.stack([f[f"ffn_mu_{n}"].reshape(chunks, P).T for n in "rk"], axis=1),
    }
    laid = {k: np.ascontiguousarray(v) for k, v in laid.items()}
    nc = bacc.Bacc("TRN2", target_bir_lowering=False, num_devices=1)
    aps = {k: nc.dram_tensor(f"in_{k}", v.shape, F32, kind="ExternalInput").ap() for k, v in laid.items()}
    out = nc.dram_tensor("out", (B * S, D), F32, kind="ExternalOutput").ap()
    v_scr = nc.dram_tensor("v_scr", (B, pairs, P, S // P, P), F32, kind="Internal").ap()
    c_scr = nc.dram_tensor("c_scr", (B, S // P, P, pairs, P), F32, kind="Internal").ap()
    attention_ffn_block(nc, out=out, v_scr=v_scr, c_scr=c_scr, **aps)
    r = run(nc, [{f"in_{k}": v for k, v in laid.items()}], core_ids=[0])
    return r.results[0]["out"].reshape(B, S, D)
```

```python
from contextlib import ExitStack

import concourse.bass as bass
from concourse import mybir

F32 = mybir.dt.float32
F32R = mybir.dt.float32r
ALU = mybir.AluOpType
ACT = mybir.ActivationFunctionType
AX = mybir.AxisListType

P = 128
HALF = 512
EPS = 1e-5


def attention_ffn_block(nc, x, wqk, bqk, wv, vb, wl, lb, ffn, mu, out, v_scr, c_scr):
    tokens, D = x.shape
    PAIRS = wqk.shape[0] - 1
    HP = PAIRS * P
    Dh = P // 2
    S = 1024
    B = tokens // S
    KT = S // P
    DC = D // P
    SLOTS = B * PAIRS
    assert PAIRS == 8 and KT == 8 and DC == 2 and S == 2 * HALF and B >= 3

    x_tiles = x.rearrange("(n p) d -> n p d", p=P)
    v_scr_slots = v_scr.rearrange("b g p k c -> (b g) p k c")
    c_scr_tiles = c_scr.rearrange("b t r g c -> (b t) r g c")
    out_tiles = out.rearrange("(n p) d -> n p d", p=P)

    with ExitStack() as ctx:
        def sb(name, shape, dt=F32):
            return ctx.enter_context(nc.sbuf_tensor(name, shape, dt))

        def sem(name):
            return ctx.enter_context(nc.semaphore(name))

        wv_hi, wv_lo = sb("wv_hi", [P, DC, HP], F32R), sb("wv_lo", [P, DC, HP], F32R)
        wl_hi, wl_lo = sb("wl_hi", [P, PAIRS, D], F32R), sb("wl_lo", [P, PAIRS, D], F32R)
        ffn_hi, ffn_lo = sb("ffn_hi", [P, 3, DC, D], F32R), sb("ffn_lo", [P, 3, DC, D], F32R)
        xt_hi, xt_lo = sb("xt_hi", [P, 2, DC, S], F32R), sb("xt_lo", [P, 2, DC, S], F32R)
        q_st = sb("q_st", [P, 2, 2, S], F32R)
        k_st = sb("k_st", [P, 2, 2, S], F32R)
        k_sw = sb("k_sw", [P, 2, 2, S], F32R)
        e_ring = sb("e_ring", [P, 4, S])
        qk_f = sb("qk_f", [P, 2, HALF])
        q_lo = sb("q_lo", [P, S], F32R)
        v_pair = sb("v_pair", [P, 2, KT, P])
        v_scaled = sb("v_scaled", [P, 2, P])
        v_out = sb("v_out", [P, HP])
        v_bias = sb("v_bias", [P, HP])
        c_out = sb("c_out", [P, S])
        c_in = sb("c_in", [P, PAIRS, P])
        c_hi, c_lo = sb("c_hi", [P, PAIRS, P], F32R), sb("c_lo", [P, PAIRS, P], F32R)
        w_raw = sb("w_raw", [P, DC, 2 * P])
        w_hi, w_lo = sb("w_hi", [P, DC, 2 * P], F32R), sb("w_lo", [P, DC, 2 * P], F32R)
        x_n = sb("x_n", [P, D])
        xn_hi, xn_lo = sb("xn_hi", [P, DC, P], F32R), sb("xn_lo", [P, DC, P], F32R)
        att = sb("att", [P, D])
        x1 = sb("x1", [P, 2, D])
        y_t = sb("y_t", [P, DC, P + 1])
        mix = sb("mix", [P, 2, DC, P])
        mix_hi, mix_lo = sb("mix_hi", [P, 2, DC, P], F32R), sb("mix_lo", [P, 2, DC, P], F32R)
        k_sq = sb("k_sq", [P, DC, P])
        ka_hi, ka_lo = sb("ka_hi", [P, DC, P], F32R), sb("ka_lo", [P, DC, P], F32R)
        gate, ff = sb("gate", [P, D]), sb("ff", [P, D])
        l_bias = sb("l_bias", [P, D])
        ident = sb("ident", [P, P])
        qk_bias = sb("qk_bias", [P, 2, PAIRS + 1])
        mu_sb = sb("mu_sb", [P, 2, DC])
        not_first = sb("not_first", [P, KT + 1])
        neg_half = sb("neg_half", [P, 1])
        neg_max = sb("neg_max", [P, 2, 2])
        e_sum, e_inv = sb("e_sum", [P, 2, 2]), sb("e_inv", [P, 2, 2])
        stats = sb("stats", [P, 4, 6])
        mean_var = sb("mean_var", [P, 4, 2])
        var_eps, rstd = sb("var_eps", [P, 4]), sb("rstd", [P, 4])
        eps = sb("eps", [P, 1])
        first_stats, first_mean = sb("first_stats", [P, KT, 6]), sb("first_mean", [P, KT, 2])
        first_eps, first_rstd = sb("first_eps", [P, KT]), sb("first_rstd", [P, KT])
        LN_IN, LN_ATT, LN_X1, LN_FF = range(4)

        score = [ctx.enter_context(nc.psum_tensor(f"score{h}", [P, S], F32)) for h in range(2)]
        context = ctx.enter_context(nc.psum_tensor("context", [P, S], F32))
        side = [ctx.enter_context(nc.psum_tensor(f"side{j}", [P, HALF], F32)) for j in range(2)]

        def sems(names):
            return [sem(n) for n in names.split()]

        bias_dma, wv_dma, wl_dma, ffn_dma, pool_ready, wv_high, wv_split, weights_high, weights_split = sems(
            "bias_dma wv_dma wl_dma ffn_dma pool_ready wv_high wv_split weights_high weights_split")
        bias_ready = sem("bias_ready")
        first_x_dma = sems("first_x_dma0 first_x_dma1")
        first_v_dma = sems("first_v_dma0 first_v_dma1")
        first_moments, first_power, first_norm, first_t, first_high, first_low, first_v, first_out = sems(
            "first_moments first_power first_norm first_t first_high first_low first_v first_out")
        scores_done, context_done, xn_transposed, v_done, qk_done = sems(
            "scores_done context_done xn_transposed v_done qk_done")
        att_done, y_transposed, ffk_done, ffr_done, ffv_done = sems(
            "att_done y_transposed ffk_done ffr_done ffv_done")
        max_done, inv_done, in_step, c_hi_done, post_step, mix_step, tail_step = sems(
            "max_done inv_done in_step c_hi_done post_step mix_step tail_step")
        exp_done, f_done, hi_done, w_hi_done, xt_done, y_step, ff_step, c_out_done = sems(
            "exp_done f_done hi_done w_hi_done xt_done y_step ff_step c_out_done")
        v_scaled_done, lo_first, lo_done, w_lo_done, c_lo_done, ka_lo_done, mix_lo_done = sems(
            "v_scaled_done lo_first lo_done w_lo_done c_lo_done ka_lo_done mix_lo_done")
        rstd_in, rstd_att, rstd_x1, rstd_ff = sems("rstd_in rstd_att rstd_x1 rstd_ff")
        x_in_dma, w_raw_dma, x_res_dma, c_in_dma, v_pair_dma, v_out_dma, q_dma = sems(
            "x_in_dma w_raw_dma x_res_dma c_in_dma v_pair_dma v_out_dma q_dma")
        k_dma = sems("k_dma0 k_dma1")
        c_out_dma, out_dma = sems("c_out_dma out_dma")

        IN = "stats mean norm high low v0 v1".split()
        POST = "bias stats mean norm x1 x1_stats x1_mean y".split()
        MIX = "diff mix high".split()
        TAIL = "square high gate product stats mean norm out".split()
        FF = "relu exp sum".split()
        AHEAD = {
            "pe": ((context_done, 2), (xn_transposed, 1), (v_done, 2), (qk_done, 4), (att_done, 1),
                   (y_transposed, 1), (ffr_done, 1), (ffv_done, 1)),
            "dve": ((in_step, len(IN)), (post_step, len(POST)), (mix_step, len(MIX)), (tail_step, 2 * len(TAIL))),
            "act": ((exp_done, 2), (xt_done, 1), (c_out_done, 1)),
            "pool": ((v_scaled_done, 8), (lo_done, 2), (w_lo_done, 1), (c_lo_done, 1), (ka_lo_done, 1)),
            "sp": ((v_out_dma, 16), (q_dma, 32), (c_out_dma, 16), (out_dma, 16)),
        }

        sp_passed, pool_passed, act_passed, dve_passed = sems("sp_passed pool_passed act_passed dve_passed")

        def exp_at(i, kt, h):
            return i * 16 + (kt * 2 + h + 3)

        def context_at(i, kt):
            return i * 8 + (kt + 3)

        def in_at(i, step):
            return i * len(IN) + (IN.index(step) + 1 + len(IN))

        def post_at(n, step):
            return n * len(POST) + (POST.index(step) + 1 + len(POST))

        def mix_at(n, step):
            return n * len(MIX) + (MIX.index(step) + 1 + len(MIX))

        def tail_at(n, step):
            return n * len(TAIL) + (TAIL.index(step) + 1 + 2 * len(TAIL))

        def ff_at(n, step):
            return n * len(FF) + (FF.index(step) + 1)

        def y_at(n, step):
            return n * 2 + step

        QK = (("k", 0), ("q", 0), ("q", 1), ("k", 1))

        def f_at(n, u):
            return n * 4 + (u + 1)

        def hi_at(n, u):
            return n * 4 + (u + 1)

        def lo_at(n, u):
            return n * 4 + (u + 3)

        def qk_at(n, u):
            return n * 4 + (u + 5)

        def v_at(i, c):
            return i * 2 + (c + 3)

        class Slot:

            def __init__(self, i, b, p, par, qk=True, pre=True, post=True, tail=True, more=True):
                self.i, self.b, self.p, self.par, self.more = i, b, p, par, more
                self.qk, self.pre, self.post, self.tail = qk, pre, post, tail

        def walk(fori, first_tiles, slot, last_slot):
            first_tiles()
            with fori(0, 4) as q:
                for par in range(2):
                    slot(Slot(q * 2 + par, 0, q * 2 + par, par, post=False, tail=False))
            slot(Slot(8, 1, 0, 0, tail=False))
            slot(Slot(9, 1, 1, 1))
            with fori(0, 3) as q:
                for par in range(2):
                    slot(Slot(q * 2 + (10 + par), 1, q * 2 + (2 + par), par))
            with fori(2, B - 1) as b:
                with fori(0, 4) as q:
                    for par in range(2):
                        slot(Slot(b * 8 + q * 2 + par, b, q * 2 + par, par))
            first = SLOTS - 8
            with fori(0, 3) as q:
                for par in range(2):
                    slot(Slot(q * 2 + (first + par), B - 1, q * 2 + par, par, pre=False))
            slot(Slot(first + 6, B - 1, 6, 0, pre=False))
            slot(Slot(first + 7, B - 1, 7, 1, pre=False, qk=False, more=False))
            last_slot(first, first - 1, None, 1)
            with fori(0, 3) as q:
                for par in range(2):
                    last_slot(q * 2 + (first + 1 + par), q * 2 + (first + par), q * 2 + (first - 1 + par), par)
            last_slot(first + 7, first + 6, first + 5, 0, more=False)
            last_slot(None, SLOTS - 1, SLOTS - 2, 1)
            last_slot(None, None, SLOTS - 1, 0)

        def halves(c):
            return slice(c * HALF, (c + 1) * HALF)

        def head_rows(h):
            return slice(h * Dh, (h + 1) * Dh)

        raw = e_ring[:, :, :].rearrange("p a c -> p (a c)")
        raw_wl = raw[:, 0:2 * S].rearrange("p (g d) -> p g d", d=D)
        raw_ffn = raw[:, 2 * S:2 * S + 3 * DC * D].rearrange("p (w c) -> p w c", w=3)
        raw_x = raw[:, 2 * S:4 * S].rearrange("p (t d) -> p t d", d=D)

        def first_tile(t):
            return raw_x[:, t, :]

        def first_bank(t, c):
            return (context, score[1])[t % 2][:, halves(c)]

        def first_transposed(t):
            bank = side[t - 6][:, :] if t >= 6 else (score[0], score[1], context)[t // 2][:, halves(t % 2)]
            return bank[:, 0:D]

        SIDE0, SIDE1, LAST_K, LAST_R, LAST_Y = range(5)
        banks = [side[0][:, :], side[1][:, :], context[:, 0:HALF], context[:, HALF:S], score[0][:, 0:HALF]]

        def context_parts(odd):
            if odd:
                return [t[:, B % 2, 0, :].rearrange("p (g c) -> p g c", c=P) for t in (xt_hi, xt_lo)]
            return c_hi[:, :, :], c_lo[:, :, :]

        OUT_PARTS = ((0, 2), (2, 5), (5, 8))

        block = ctx.enter_context(nc.Block())

        @block.sync
        def _(sp):
            for s, n in AHEAD["sp"]:
                sp.sem_inc(s, n)
            for g in range(2):
                sp.dma_start(first_tile(slice(4 * g, 4 * g + 4)),
                             x_tiles[4 * g:4 * g + 4].rearrange("n p d -> p n d")).then_inc(first_x_dma[g], 16)
            sp.dma_start(e_ring[:, 0:2, :], wv).then_inc(wv_dma, 16)
            sp.dma_start(v_bias[:, :], vb.partition_broadcast(P)).then_inc(bias_dma, 16)
            sp.dma_start(qk_bias[:, :, :], bqk).then_inc(bias_dma, 16)
            sp.dma_start(l_bias[:, :], lb.partition_broadcast(P)).then_inc(bias_dma, 16)
            sp.dma_start(mu_sb[:, :, :], mu).then_inc(bias_dma, 16)

            def load_x(i):
                sp.wait_ge(xn_transposed, i + 1)
                sp.sem_inc(sp_passed, 1)
                sp.dma_start(x_n[:, :], x_tiles[i + 8]).then_inc(x_in_dma, 16)

            def load_w(n, pair):
                sp.wait_ge(w_lo_done, n + 1)
                sp.sem_inc(sp_passed, 1)
                sp.dma_start(w_raw[:, :, :], wqk[pair]).then_inc(w_raw_dma, 16)

            def store_v(i, b, t):
                sp.wait_ge(in_step, in_at(i, "v1"))
                sp.sem_inc(sp_passed, 1)
                sp.dma_start(v_scr[b, :, :, t, :].rearrange("g p c -> p g c"),
                             v_out[:, :].rearrange("p (g c) -> p g c", c=P)).then_inc(v_out_dma, 16)

            def load_v(i, par):
                sp.wait_ge(v_scaled_done, i * 8)
                sp.sem_inc(sp_passed, 1)
                sp.dma_start(v_pair[:, par, :, :], v_scr_slots[i]).then_inc(v_pair_dma, 16)

            def move_q(n, par):
                sp.wait_ge(lo_first, n * 4 + 3)
                sp.sem_inc(sp_passed, 1)
                sp.dma_start(q_st[Dh:P, par, 0, :].bitcast(F32), q_lo[0:Dh, :].bitcast(F32)).then_inc(q_dma, 16)
                sp.wait_ge(lo_done, lo_at(n, 2))
                sp.sem_inc(sp_passed, 1)
                sp.dma_start(q_st[0:Dh, par, 1, :].bitcast(F32), q_lo[Dh:P, :].bitcast(F32)).then_inc(q_dma, 16)

            def move_k(n, par, c):
                sp.wait_ge(lo_done, lo_at(n, QK.index(("k", c))))
                sp.sem_inc(sp_passed, 1)
                for dst, src in ((k_st, k_sw), (k_sw, k_st)):
                    sp.dma_start(dst[Dh:P, par, 0, halves(c)].bitcast(F32),
                                 src[0:Dh, par, 0, halves(c)].bitcast(F32)).then_inc(k_dma[c], 16)
                    sp.dma_start(dst[0:Dh, par, 1, halves(c)].bitcast(F32),
                                 src[Dh:P, par, 1, halves(c)].bitcast(F32)).then_inc(k_dma[c], 16)

            def load_context(n, stored):
                sp.wait_ge(c_lo_done, n + 1)
                sp.sem_inc(sp_passed, 1)
                sp.wait_ge(c_out_dma, stored)
                sp.sem_inc(sp_passed, 1)
                sp.dma_start(c_in[:, :, :], c_scr_tiles[n]).then_inc(c_in_dma, 16)

            def load_residual(n, par):
                sp.wait_ge(tail_step, tail_at(n - 2, "out"))
                sp.sem_inc(sp_passed, 1)
                sp.dma_start(x1[:, par, :], x_tiles[n]).then_inc(x_res_dma, 16)

            def first_tiles():
                load_w(0, 0)
                sp.wait_ge(wv_split, 1)
                sp.dma_start(e_ring[:, 0:2, :], wl).then_inc(wl_dma, 16)
                sp.wait_ge(first_t, KT)
                sp.dma_start(raw_ffn, ffn).then_inc(ffn_dma, 16)
                for t in range(KT):
                    sp.wait_ge(first_out, 2 * t + 2)
                    sp.dma_start(v_scr[0, :, :, t, :].rearrange("g p c -> p g c"),
                                 (v_out, c_out)[t % 2][:, :].rearrange("p (g c) -> p g c", c=P)
                                 ).then_inc(first_v_dma[t % 2], 16)
                    if t == 1:
                        move_k(0, 0, 0)
                    if t == 4:
                        move_q(0, 0)
                for d in first_v_dma:
                    sp.wait_ge(d, 16 * KT // 2)
                load_v(0, 0)

            def slot(s):
                if s.pre:
                    load_x(s.i)
                if s.qk:
                    load_w(s.i + 1, s.p + 1)
                if s.post:
                    load_context(s.i - 8, s.b * 128 + 16)
                    load_residual(s.i - 8, s.par)
                move_k(s.i, s.par, 1)
                if s.pre:
                    store_v(s.i, s.b + 1, s.p)
                    sp.wait_ge(v_out_dma, s.i * 16 + 32)
                    sp.sem_inc(sp_passed, 1)
                if s.more:
                    load_v(s.i + 1, 1 - s.par)
                if s.qk:
                    move_k(s.i + 1, 1 - s.par, 0)
                    move_q(s.i + 1, 1 - s.par)

            def last_slot(n, a, o, par, more=True):
                if n is not None and o is None:
                    load_context(n, 16 * SLOTS + 16)
                if n is not None and more:
                    load_context(n + 1, 16 * SLOTS + 16)
                if n is not None:
                    sp.wait_ge(post_step, post_at(a, "x1"))
                    sp.sem_inc(sp_passed, 1)
                    sp.dma_start(x_n[:, :], x_tiles[n]).then_inc(x_res_dma, 16)

            walk(sp.Fori, first_tiles, slot, last_slot)
            sp.wait_ge(out_dma, 16 * (SLOTS + 1))
            sp.wait_ge(v_out_dma, 16 * (SLOTS - 7))
            sp.wait_ge(c_out_dma, 16 * (SLOTS + 1))

        @block.gpsimd
        def _(pool):
            for s, n in AHEAD["pool"]:
                pool.sem_inc(s, n)
            pool.memset(neg_half[:, :], -0.5)
            pool.memset(eps[:, :], EPS)
            pool.memset(not_first[:, :], 1.0)
            pool.memset(ident[:, :], 0.0).then_inc(pool_ready, 1)
            pool.wait_ge(pool_ready, 1)
            pool.affine_select(out=ident[:, :], in_=ident[:, :], compare_op=ALU.not_equal, fill=1.0, base=0,
                               pattern=[[-1, P]], channel_multiplier=1)
            pool.memset(not_first[:, 1:2], 0.0).then_inc(pool_ready, 1)
            pool.wait_ge(pool_ready, 2)

            def low(out, full, high):
                return pool.tensor_tensor(out, full, high.bitcast(F32), ALU.subtract)

            def power(row, sem_, at, done, n):
                pool.wait_ge(sem_, at)
                pool.sem_inc(pool_passed, 1)
                pool.tensor_tensor(var_eps[:, row:row + 1], mean_var[:, row, 1:2], eps[:, :], ALU.add).then_inc(done, 1)
                pool.wait_ge(done, n * 2 + 1)
                pool.sem_inc(pool_passed, 1)
                pool.tensor_tensor(rstd[:, row:row + 1], var_eps[:, row:row + 1], neg_half[:, :],
                                   ALU.pow).then_inc(done, 1)

            def split_w(n):
                pool.wait_ge(w_hi_done, n + 1)
                pool.sem_inc(pool_passed, 1)
                pool.wait_ge(qk_done, qk_at(n - 1, 3))
                pool.sem_inc(pool_passed, 1)
                low(w_lo[:, :, :], w_raw[:, :, :], w_hi[:, :, :]).then_inc(w_lo_done, 1)

            def split_qk(n, par, u):
                pool.wait_ge(hi_done, hi_at(n, u))
                pool.sem_inc(pool_passed, 1)
                kind, c = QK[u]
                if u == 1:
                    pool.wait_ge(q_dma, n * 32 + 32)
                    pool.sem_inc(pool_passed, 1)
                for h, done in enumerate((lo_first, lo_done)):
                    rows = head_rows(h)
                    if kind == "q":
                        low(q_lo[rows, halves(c)], qk_f[rows, u % 2, :],
                            q_st[rows, par, h, halves(c)]).then_inc(done, 1)
                    else:
                        low(k_sw[rows, par, h, halves(c)], qk_f[rows, u % 2, :],
                            k_st[rows, par, h, halves(c)]).then_inc(done, 1)
                    pool.wait_ge(done, n * 4 + (u + 1) if h == 0 else lo_at(n, u))
                    pool.sem_inc(pool_passed, 1)

            def scale_v(s, kt):
                pool.wait_ge(inv_done, s.i * 8 + (kt + 1))
                pool.sem_inc(pool_passed, 1)
                if kt == 0:
                    pool.wait_ge(v_pair_dma, s.i * 16 + 16)
                    pool.sem_inc(pool_passed, 1)
                pool.tensor_tensor(v_scaled[:, kt % 2, :].rearrange("p (h c) -> p h c", h=2),
                                   v_pair[:, s.par, kt, :].rearrange("p (h c) -> p h c", h=2),
                                   e_inv[:, kt % 2, :].unsqueeze(2).broadcast_to([P, 2, Dh]),
                                   ALU.mult).then_inc(v_scaled_done, 1)

            def split_context(n, last=False, odd=0):
                c_hi, c_lo = context_parts(odd)
                pool.wait_ge(c_hi_done, n + 1)
                pool.sem_inc(pool_passed, 1)
                pool.wait_ge(att_done, n if last else n + 1)
                pool.sem_inc(pool_passed, 1)
                low(c_lo, c_in[:, :, :], c_hi).then_inc(c_lo_done, 1)

            def split_ka(n):
                pool.wait_ge(tail_step, tail_at(n, "high"))
                pool.sem_inc(pool_passed, 1)
                low(ka_lo[:, :, :], k_sq[:, :, :], ka_hi[:, :, :]).then_inc(ka_lo_done, 1)

            def split_mix(n):
                pool.wait_ge(mix_step, mix_at(n, "high"))
                pool.sem_inc(pool_passed, 1)
                low(mix_lo[:, :, :, :], mix[:, :, :, :], mix_hi[:, :, :, :]).then_inc(mix_lo_done, 1)

            def first_tiles():
                for g in range(2):
                    tiles = slice(4 * g, 4 * g + 4)
                    pool.wait_ge(first_moments, 4 * g + 4)
                    pool.tensor_tensor(first_eps[:, tiles].unsqueeze(2), first_mean[:, tiles, 1:2],
                                       eps[:, :].unsqueeze(1).broadcast_to([P, 4, 1]),
                                       ALU.add).then_inc(first_power, 1)
                    pool.wait_ge(first_power, 2 * g + 1)
                    pool.tensor_tensor(first_rstd[:, tiles], first_eps[:, tiles], neg_half[:, :].broadcast_to([P, 4]),
                                       ALU.pow).then_inc(first_power, 1)
                split_w(0)
                for u in range(3):
                    split_qk(0, 0, u)

            def power_in(i):
                power(LN_IN, in_step, in_at(i, "mean"), rstd_in, i)

            def power_att(n):
                power(LN_ATT, post_step, post_at(n, "mean"), rstd_att, n)

            def power_x1(n):
                power(LN_X1, post_step, post_at(n, "x1_mean"), rstd_x1, n)

            def power_ff(n):
                power(LN_FF, tail_step, tail_at(n, "mean"), rstd_ff, n)

            def slot(s):
                n, o = s.i - 8, s.i - 9
                for kt in range(KT):
                    scale_v(s, kt)
                    if kt == 0 and s.tail:
                        power_att(o)
                    if kt == 0 and s.pre:
                        power_in(s.i)
                    if kt == 1 and s.tail:
                        power_x1(o)
                    if kt == 1:
                        split_qk(s.i, s.par, 3)
                    if kt == 2 and s.qk:
                        split_w(s.i + 1)
                    if kt == 2 and s.post:
                        split_context(n)
                    if kt == 3 and s.tail:
                        split_mix(o)
                    if 3 <= kt <= 5 and s.qk:
                        split_qk(s.i + 1, 1 - s.par, kt - 3)
                    if kt == 4 and s.tail:
                        split_ka(o)
                    if kt == 6 and s.tail:
                        power_ff(o)

            def last_slot(n, a, o, par, more=True):
                if n is not None and o is None:
                    split_context(n)
                if a is not None and o is None:
                    power_att(a)
                if a is not None:
                    power_x1(a)
                if o is not None:
                    split_ka(o)
                if n is not None and more:
                    split_context(n + 1, True, par)
                if a is not None:
                    split_mix(a)
                if o is not None:
                    power_ff(o)
                if n is not None:
                    power_att(n)

            walk(pool.Fori, first_tiles, slot, last_slot)

        @block.scalar
        def _(act):
            for s, n in AHEAD["act"]:
                act.sem_inc(s, n)
            act.wait_ge(bias_dma, 64)
            act.activation(qk_bias[:, 0, :], qk_bias[:, 0, :], ACT.Copy, scale=Dh ** -0.5).then_inc(bias_ready, 1)
            act.wait_ge(bias_ready, 1)

            def high_w(n):
                act.wait_ge(w_raw_dma, n * 16 + 16)
                act.wait_ge(qk_done, qk_at(n - 1, 3))
                act.activation(w_hi[:, :, :], w_raw[:, :, :], ACT.Copy).then_inc(w_hi_done, 1)

            def keep_xt(i, buf, t):
                act.wait_ge(in_step, in_at(i, "low"))
                act.sem_inc(act_passed, 1)
                for dst, src in ((xt_hi, xn_hi), (xt_lo, xn_lo)):
                    last = act.activation(dst[:, buf, :, bass.ts(t, P)], src[:, :, :].bitcast(F32), ACT.Copy)
                last.then_inc(xt_done, 1)

            def full_qk(n, pair, u):
                act.wait_ge(qk_done, qk_at(n, u))
                act.wait_ge(lo_done, lo_at(n, u - 2))
                act.sem_inc(act_passed, 1)
                act.activation(qk_f[:, u % 2, :], side[1][:, :], ACT.Identity,
                               bias=qk_bias[:, "qk".index(QK[u][0]), bass.ds(pair, 1)],
                               scale=Dh ** -0.5 if QK[u][0] == "q" else 1.0).then_inc(f_done, 1)

            def high_qk(n, par, u):
                kind, c = QK[u]
                act.wait_ge(f_done, f_at(n, u))
                for h in range(2):
                    last = act.activation((q_st if kind == "q" else k_st)[head_rows(h), par, h, halves(c)],
                                          qk_f[head_rows(h), u % 2, :], ACT.Copy)
                last.then_inc(hi_done, 1)

            def exps(i, kt):
                for h in range(2):
                    act.wait_ge(max_done, i * 16 + (kt * 2 + h + 1))
                    act.wait_ge(context_done, i * 8 + (kt + 1))
                    act.activation(e_ring[:, (2 * kt + h) % 4, :], score[h][:, :], ACT.Exp,
                                   bias=neg_max[:, kt % 2, h:h + 1],
                                   accum_out=e_sum[:, kt % 2, h:h + 1]).then_inc(exp_done, 1)

            def ff_relu(n, bank):
                act.wait_ge(ffk_done, n + 1)
                act.wait_ge(ka_lo_done, n + 1)
                act.activation(k_sq[:, :, :], banks[bank][:, 0:D].rearrange("p (c t) -> p c t", c=DC),
                               ACT.Relu).then_inc(ff_step, 1)

            def ff_gate(n, bank):
                act.wait_ge(ffr_done, n + 2)
                act.wait_ge(tail_step, tail_at(n - 1, "product"))
                act.activation(gate[:, :], banks[bank][:, 0:D], ACT.Exp, scale=-1.0).then_inc(ff_step, 1)
                act.wait_ge(ff_step, ff_at(n, "exp"))
                act.activation(gate[:, :], gate[:, :], ACT.Copy, bias=1.0).then_inc(ff_step, 1)

            def keep_y(n, t, bank):
                act.wait_ge(mix_step, mix_at(n - 1, "mix"))
                act.sem_inc(act_passed, 1)
                act.activation(y_t[:, :, 0:1], y_t[:, :, P:P + 1], ACT.Copy,
                               scale=not_first[:, bass.ds(t, 1)]).then_inc(y_step, 1)
                act.wait_ge(y_transposed, n + 2)
                act.wait_ge(y_step, y_at(n, 1))
                act.activation(y_t[:, :, 1:P + 1], banks[bank][:, 0:D].rearrange("p (c t) -> p c t", c=DC),
                               ACT.Copy).then_inc(y_step, 1)

            def keep_context(i):
                act.wait_ge(context_done, context_at(i, 7))
                act.wait_ge(c_out_dma, i * 16 + 16)
                act.activation(c_out[:, :], context[:, :], ACT.Copy).then_inc(c_out_done, 1)

            def store_context(i, b, p):
                act.wait_ge(c_out_done, i + 2)
                act.dma_start(c_scr[b, :, :, p, :].rearrange("t r c -> r t c"),
                              c_out[:, :].rearrange("r (t c) -> r t c", c=P)).then_inc(c_out_dma, 16)

            def store_out(n):
                act.wait_ge(tail_step, tail_at(n, "out"))
                act.dma_start(out_tiles[n], ff[:, :]).then_inc(out_dma, 16)

            def first_tiles():
                high_w(0)
                for t in range(KT):
                    act.wait_ge(first_t, t + 1)
                    act.activation(xt_hi[:, 0, :, bass.ts(t, P)],
                                   first_transposed(t).rearrange("p (c t) -> p c t", c=DC),
                                   ACT.Copy).then_inc(first_high, 1)
                act.wait_ge(wv_dma, 16)
                act.activation(wv_hi[:, :, :], e_ring[:, 0:2, :], ACT.Copy).then_inc(wv_high, 1)
                for u in range(3):
                    full_qk(0, 0, u)
                    high_qk(0, 0, u)
                act.wait_ge(wl_dma, 16)
                act.activation(wl_hi[:, :, :], raw_wl, ACT.Copy).then_inc(weights_high, 1)
                act.wait_ge(ffn_dma, 16)
                act.activation(ffn_hi[:, :, :, :].rearrange("p w c d -> p w (c d)"), raw_ffn,
                               ACT.Copy).then_inc(weights_high, 1)
                act.wait_ge(weights_split, 1)
                for d in first_v_dma:
                    act.wait_ge(d, 16 * KT // 2)
                exps(0, 0)

            def slot(s):
                n, o = s.i - 8, s.i - 9
                for kt in range(KT):
                    if kt == 1:
                        full_qk(s.i, s.p, 3)
                        high_qk(s.i, s.par, 3)
                    if kt == 2 and s.tail:
                        keep_y(o, s.p, SIDE0)
                    if kt == 4 and s.tail:
                        ff_relu(o, SIDE0)
                    if kt == 5 and s.tail:
                        ff_gate(o, SIDE0)
                    if 3 <= kt <= 5 and s.qk:
                        full_qk(s.i + 1, s.p + 1, kt - 3)
                        high_qk(s.i + 1, 1 - s.par, kt - 3)
                    if kt < KT - 1:
                        exps(s.i, kt + 1)
                    elif s.more:
                        exps(s.i + 1, 0)
                    if kt == 1 and s.pre:
                        keep_xt(s.i, (s.b + 1) % 2, s.p)
                    if kt == 1 and s.qk:
                        high_w(s.i + 1)
                keep_context(s.i)
                store_context(s.i, s.b, s.p)
                if s.tail:
                    store_out(o)

            def high_context(n, at, odd):
                act.wait_ge(c_in_dma, n * 16 + 16)
                act.wait_ge(att_done, at)
                act.activation(context_parts(odd)[0], c_in[:, :, :], ACT.Copy).then_inc(c_hi_done, 1)

            def last_slot(n, a, o, par, more=True):
                if n is not None and o is None:
                    high_context(n, n + 1, 0)
                if n is not None and more:
                    high_context(n + 1, n + 1, par)
                if o is not None:
                    ff_relu(o, LAST_K)
                    ff_gate(o, LAST_R)
                if a is not None:
                    keep_y(a, a - (SLOTS - 9), LAST_Y)
                if o is not None:
                    store_out(o)

            walk(act.Fori, first_tiles, slot, last_slot)

        @block.vector
        def _(dve):
            for s, n in AHEAD["dve"]:
                dve.sem_inc(s, n)
            dve.memset(y_t[:, :, :], 0.0)

            def high(out, full):
                return dve.tensor_copy(out, full)

            def low(out, full, high_part):
                return dve.tensor_tensor(out, full, high_part.bitcast(F32), ALU.subtract)

            def moments(row, src, sem_, at_src, at_stats):
                if at_src is not None:
                    dve.wait_ge(sem_, at_src)
                dve.bn_stats(stats[:, row, :], src).then_inc(sem_, 1)
                dve.wait_ge(sem_, at_stats)
                dve.sem_inc(dve_passed, 1)
                dve.bn_aggr(mean_var[:, row, :], stats[:, row, :]).then_inc(sem_, 1)

            def normalise(out, src, row):
                return dve.tensor_scalar(out, src, mean_var[:, row, 0:1], rstd[:, row:row + 1],
                                         ALU.subtract, ALU.mult)

            def in_moments(i):
                dve.wait_ge(x_in_dma, i * 16 + 16)
                moments(LN_IN, x_n[:, :], in_step, None, in_at(i, "stats"))

            def in_norm(i):
                dve.wait_ge(rstd_in, i * 2 + 2)
                normalise(x_n[:, :], x_n[:, :], LN_IN).then_inc(in_step, 1)

            def in_split(i):
                dve.wait_ge(xn_transposed, i + 2)
                dve.wait_ge(v_done, v_at(i - 1, 1))
                dve.wait_ge(xt_done, i + 1)
                xn = side[0][:, 0:D].rearrange("p (c t) -> p c t", c=DC)
                high(xn_hi[:, :, :], xn).then_inc(in_step, 1)
                dve.wait_ge(in_step, in_at(i, "high"))
                low(xn_lo[:, :, :], xn, xn_hi[:, :, :]).then_inc(in_step, 1)

            def in_v(i, c):
                dve.wait_ge(v_done, v_at(i, c))
                if c == 0:
                    dve.wait_ge(v_out_dma, i * 16 + 16)
                dve.tensor_tensor(v_out[:, halves(c)], side[1 - c][:, :], v_bias[:, halves(c)],
                                  ALU.add).then_inc(in_step, 1)

            def maxima(i, kt):
                for h in range(2):
                    dve.wait_ge(scores_done, i * 16 + (kt * 2 + h + 1))
                    dve.reduce_max(neg_max[:, kt % 2, h:h + 1], score[h][:, :], AX.X,
                                   negate=True).then_inc(max_done, 1)

            def inverse(i, kt):
                dve.wait_ge(exp_done, exp_at(i, kt, 1))
                dve.reciprocal(e_inv[:, kt % 2, :], e_sum[:, kt % 2, :]).then_inc(inv_done, 1)

            def post_high_context(n):
                dve.wait_ge(c_in_dma, n * 16 + 16)
                dve.wait_ge(att_done, n + 1)
                high(c_hi[:, :, :], c_in[:, :, :]).then_inc(c_hi_done, 1)

            def post_attention(n):
                dve.wait_ge(att_done, n + 2)
                dve.wait_ge(y_transposed, n + 1)
                dve.tensor_tensor(att[:, :], side[0][:, 0:D], l_bias[:, :], ALU.add).then_inc(post_step, 1)
                moments(LN_ATT, att[:, :], post_step, post_at(n, "bias"), post_at(n, "stats"))

            def post_residual(n, par, x_tile):
                dve.wait_ge(rstd_att, n * 2 + 2)
                normalise(att[:, :], att[:, :], LN_ATT).then_inc(post_step, 1)
                dve.wait_ge(x_res_dma, n * 16 + 16)
                dve.wait_ge(post_step, post_at(n, "norm"))
                dve.tensor_tensor(x1[:, par, :], att[:, :], x_tile, ALU.add).then_inc(post_step, 1)
                moments(LN_X1, x1[:, par, :], post_step, post_at(n, "x1"), post_at(n, "x1_stats"))

            def post_y(n, par):
                dve.wait_ge(rstd_x1, n * 2 + 2)
                normalise(att[:, :], x1[:, par, :], LN_X1).then_inc(post_step, 1)

            def post_mix(n):
                dve.wait_ge(y_step, y_at(n, 2))
                dve.wait_ge(ffr_done, n + 1)
                dve.tensor_tensor(mix[:, 1, :, :], y_t[:, :, 1:P + 1], y_t[:, :, 0:P],
                                  ALU.subtract).then_inc(mix_step, 1)
                dve.wait_ge(mix_step, mix_at(n, "diff"))
                for w in range(2):
                    for c in range(DC):
                        last = dve.scalar_tensor_tensor(mix[:, w, c, :], mix[:, 1, c, :], mu_sb[:, w, c:c + 1],
                                                        y_t[:, c, 0:P], ALU.mult, ALU.add)
                last.then_inc(mix_step, 1)
                dve.wait_ge(mix_step, mix_at(n, "mix"))
                high(mix_hi[:, :, :, :], mix[:, :, :, :]).then_inc(mix_step, 1)

            def tail_square(n):
                dve.wait_ge(ff_step, ff_at(n, "relu"))
                dve.tensor_tensor(k_sq[:, :, :], k_sq[:, :, :], k_sq[:, :, :], ALU.mult).then_inc(tail_step, 1)
                dve.wait_ge(tail_step, tail_at(n, "square"))
                dve.wait_ge(ffv_done, n + 1)
                high(ka_hi[:, :, :], k_sq[:, :, :]).then_inc(tail_step, 1)

            def tail_gate(n):
                dve.wait_ge(ff_step, ff_at(n, "sum"))
                dve.reciprocal(gate[:, :], gate[:, :]).then_inc(tail_step, 1)

            def tail_product(n, bank):
                dve.wait_ge(ffv_done, n + 2)
                dve.wait_ge(out_dma, n * 16 + 16)
                dve.wait_ge(tail_step, tail_at(n, "gate"))
                dve.tensor_tensor(ff[:, :], banks[bank][:, 0:D], gate[:, :], ALU.mult).then_inc(tail_step, 1)
                moments(LN_FF, ff[:, :], tail_step, tail_at(n, "product"), tail_at(n, "stats"))

            def tail_out(n, par):
                dve.wait_ge(rstd_ff, n * 2 + 2)
                normalise(ff[:, :], ff[:, :], LN_FF).then_inc(tail_step, 1)
                dve.wait_ge(tail_step, tail_at(n, "norm"))
                dve.tensor_tensor(ff[:, :], ff[:, :], x1[:, par, :], ALU.add).then_inc(tail_step, 1)

            def first_tiles():
                for t in range(KT):
                    if t % 4 == 0:
                        dve.wait_ge(first_x_dma[t // 4], 16)
                    dve.bn_stats(first_stats[:, t, :], first_tile(t)).then_inc(first_norm, 1)
                for t in range(KT):
                    dve.wait_ge(first_norm, KT)
                    dve.bn_aggr(first_mean[:, t, :], first_stats[:, t, :]).then_inc(first_moments, 1)
                for t in range(KT):
                    if t % 4 == 0:
                        dve.wait_ge(first_power, t // 2 + 2)
                    dve.wait_ge(first_moments, KT)
                    dve.tensor_scalar(first_tile(t), first_tile(t), first_mean[:, t, 0:1], first_rstd[:, t:t + 1],
                                      ALU.subtract, ALU.mult).then_inc(first_norm, 1)
                for t in range(KT):
                    dve.wait_ge(first_high, t + 1)
                    low(xt_lo[:, 0, :, bass.ts(t, P)], first_transposed(t).rearrange("p (c t) -> p c t", c=DC),
                        xt_hi[:, 0, :, bass.ts(t, P)]).then_inc(first_low, 1)
                dve.wait_ge(wv_high, 1)
                low(wv_lo[:, :, :], e_ring[:, 0:2, :], wv_hi[:, :, :]).then_inc(wv_split, 1)
                dve.wait_ge(bias_dma, 64)
                for t in range(KT):
                    if t >= 2:
                        dve.wait_ge(first_v_dma[t % 2], 16 * (t // 2))
                    for c in range(2):
                        dve.wait_ge(first_v, 2 * t + c + 1)
                        dve.tensor_tensor((v_out, c_out)[t % 2][:, halves(c)], first_bank(t, c),
                                          v_bias[:, halves(c)], ALU.add).then_inc(first_out, 1)
                    if t == 4:
                        dve.wait_ge(weights_high, 1)
                        low(wl_lo[:, :, :], raw_wl, wl_hi[:, :, :])
                    if t == 5:
                        dve.wait_ge(weights_high, 2)
                        low(ffn_lo[:, :, :, :].rearrange("p w c d -> p w (c d)"), raw_ffn,
                            ffn_hi[:, :, :, :].rearrange("p w c d -> p w (c d)")).then_inc(weights_split, 1)
                maxima(0, 0)

            def slot(s):
                n, o = s.i - 8, s.i - 9
                for kt in range(KT):
                    inverse(s.i, kt)
                    if kt == 0 and s.tail:
                        post_attention(o)
                    if kt == 0 and s.pre:
                        in_moments(s.i)
                    if kt == 1 and s.pre:
                        in_split(s.i)
                    if kt == 2 and s.pre:
                        in_v(s.i, 0)
                    if kt == 2 and s.post:
                        post_high_context(n)
                    if kt == 3 and s.pre:
                        in_v(s.i, 1)
                    if kt == 6 and s.tail:
                        tail_product(o, SIDE1)
                    if kt == 7 and s.tail:
                        tail_out(o, 1 - s.par)
                    if kt < KT - 1:
                        maxima(s.i, kt + 1)
                    elif s.more:
                        maxima(s.i + 1, 0)
                    if kt == 0 and s.pre:
                        in_norm(s.i)
                    if kt == 0 and s.tail:
                        post_residual(o, 1 - s.par, x1[:, 1 - s.par, :])
                    if kt == 1 and s.tail:
                        post_y(o, 1 - s.par)
                    if kt == 2 and s.tail:
                        post_mix(o)
                    if kt == 4 and s.tail:
                        tail_square(o)
                    if kt == 5 and s.tail:
                        tail_gate(o)

            def last_slot(n, a, o, par, more=True):
                if a is not None and o is None:
                    post_attention(a)
                if a is not None:
                    post_residual(a, par, x1[:, par, :] if o is None else x_n[:, :])
                if o is not None:
                    tail_square(o)
                if a is not None:
                    post_y(a, par)
                if o is not None:
                    tail_gate(o)
                if a is not None:
                    post_mix(a)
                if o is not None:
                    tail_product(o, SIDE1)
                if n is not None:
                    post_attention(n)
                if o is not None:
                    tail_out(o, 1 - par)

            walk(dve.Fori, first_tiles, slot, last_slot)

        @block.tensor
        def _(pe):
            for s, n in AHEAD["pe"]:
                pe.sem_inc(s, n)

            busy = [[] for _ in banks]

            def take(bank, *freed):
                for done, at in busy[bank]:
                    pe.wait_ge(done, at)
                busy[bank] = list(freed)

            def split_product(out, pairs, first=True, last=True):
                terms = [t for a_hi, a_lo, b_hi, b_lo in pairs
                         for t in ((a_hi, b_hi), (a_hi, b_lo), (a_lo, b_hi))]
                for k, (a, b) in enumerate(terms):
                    mm = pe.matmul(out, a, b, start=first and k == 0, stop=last and k == len(terms) - 1)
                return mm

            def transpose_xn(i):
                take(0, (in_step, in_at(i, "low")))
                pe.wait_ge(in_step, in_at(i, "norm"))
                for c in range(DC):
                    mm = pe.transpose(side[0][:, bass.ts(c, P)], x_n[:, bass.ts(c, P)], ident[:, :])
                mm.then_inc(xn_transposed, 1)

            def project_v(i, c):
                take(1 - c, (in_step, in_at(i, ("v0", "v1")[c])))
                pe.wait_ge(in_step, in_at(i, "low"))
                split_product(side[1 - c][:, :],
                              [(xn_hi[:, k, :], xn_lo[:, k, :], wv_hi[:, k, halves(c)], wv_lo[:, k, halves(c)])
                               for k in range(DC)]).then_inc(v_done, 1)

            def project_qk(n, u):
                take(1, (f_done, f_at(n, u)))
                if u == 0:
                    pe.wait_ge(w_lo_done, n + 2)
                    pe.wait_ge(xt_done, (n // 8) * 8 + 1)
                kind, half = QK[u]
                w = slice(0, P) if kind == "q" else slice(P, 2 * P)
                buf = (n // 8) % 2
                split_product(side[1][:, :],
                              [(w_hi[:, k, w], w_lo[:, k, w], xt_hi[:, buf, k, halves(half)],
                                xt_lo[:, buf, k, halves(half)]) for k in range(DC)]).then_inc(qk_done, 1)

            def scores(i, par, kt):
                if kt == 0:
                    pe.wait_ge(q_dma, i * 32 + 64)
                    pe.wait_ge(k_dma[0], i * 64 + 64)
                if kt == KT // 2:
                    pe.wait_ge(k_dma[1], i * 64 + 64)
                for h in range(2):
                    pe.wait_ge(exp_done, i * 16 + (kt * 2 + h + 1))
                    for c in range(2):
                        for k in (k_st, k_sw):
                            mm = pe.matmul(score[h][:, halves(c)], k[:, par, h, bass.ts(kt, P)],
                                           q_st[:, par, h, halves(c)], start=k is k_st, stop=k is k_sw)
                    mm.then_inc(scores_done, 1)

            def weighted(i, kt):
                if kt == 0:
                    pe.wait_ge(c_out_done, i + 1)
                pe.wait_ge(v_scaled_done, i * 8 + (kt + 9))
                for c in range(2):
                    for h in range(2):
                        mm = pe.matmul(context[head_rows(h), halves(c)], v_scaled[:, kt % 2, head_rows(h)],
                                       e_ring[:, (2 * kt + h) % 4, halves(c)], start=kt == 0, stop=kt == KT - 1)
                mm.then_inc(context_done, 1)

            def project_out(n, part, odd=0):
                c_hi, c_lo = context_parts(odd)
                if part == 0:
                    take(SIDE0, (post_step, post_at(n, "bias")))
                    pe.wait_ge(c_lo_done, n + 2)
                mm = split_product(side[0][:, 0:D],
                                   [(c_hi[:, g, :], c_lo[:, g, :], wl_hi[:, g, :], wl_lo[:, g, :])
                                    for g in range(*OUT_PARTS[part])], first=part == 0, last=part == 2)
                if part == 2:
                    mm.then_inc(att_done, 1)

            def transpose_y(n, bank):
                take(bank, (y_step, y_at(n, 2)))
                pe.wait_ge(post_step, post_at(n, "y"))
                for c in range(DC):
                    mm = pe.transpose(banks[bank][:, bass.ts(c, P)], att[:, bass.ts(c, P)], ident[:, :])
                mm.then_inc(y_transposed, 1)

            def feed_k(n, bank):
                take(bank, (ff_step, ff_at(n, "relu")))
                pe.wait_ge(mix_lo_done, n + 1)
                for d in range(DC):
                    mm = split_product(banks[bank][:, bass.ts(d, P)],
                                       [(ffn_hi[:, 1, c, bass.ts(d, P)], ffn_lo[:, 1, c, bass.ts(d, P)],
                                         mix_hi[:, 1, c, :], mix_lo[:, 1, c, :]) for c in range(DC)])
                mm.then_inc(ffk_done, 1)

            def feed_r(n, bank):
                take(bank, (ff_step, ff_at(n, "exp")))
                split_product(banks[bank][:, 0:D],
                              [(mix_hi[:, 0, c, :], mix_lo[:, 0, c, :], ffn_hi[:, 0, c, :], ffn_lo[:, 0, c, :])
                               for c in range(DC)]).then_inc(ffr_done, 1)

            def feed_v(n, bank):
                take(bank, (tail_step, tail_at(n, "product")))
                pe.wait_ge(ka_lo_done, n + 2)
                split_product(banks[bank][:, 0:D],
                              [(ka_hi[:, c, :], ka_lo[:, c, :], ffn_hi[:, 2, c, :], ffn_lo[:, 2, c, :])
                               for c in range(DC)]).then_inc(ffv_done, 1)

            def first_tiles():
                pe.wait_ge(pool_ready, 2)

                for t in range(KT):
                    pe.wait_ge(first_norm, KT + t + 1)
                    for c in range(DC):
                        mm = pe.transpose(first_transposed(t)[:, bass.ts(c, P)], first_tile(t)[:, bass.ts(c, P)],
                                          ident[:, :])
                    mm.then_inc(first_t, 1)
                pe.wait_ge(first_low, KT)
                for u in range(3):
                    project_qk(0, u)
                pe.wait_ge(wv_split, 1)
                for t in range(KT):
                    for c in range(2):
                        if t >= 2:
                            pe.wait_ge(first_out, 2 * (t - 2) + c + 1)
                        split_product(first_bank(t, c),
                                      [(xt_hi[:, 0, k, bass.ts(t, P)], xt_lo[:, 0, k, bass.ts(t, P)],
                                        wv_hi[:, k, halves(c)], wv_lo[:, k, halves(c)])
                                       for k in range(DC)]).then_inc(first_v, 1)
                pe.wait_ge(first_out, 2 * KT)
                scores(0, 0, 0)

            def slot(s):
                n, o = s.i - 8, s.i - 9
                busy[SIDE0] = [(post_step, post_at(o, "bias")) if s.tail else (in_step, in_at(s.i - 1, "v1"))]
                busy[SIDE1] = [(f_done, f_at(s.i, 2))]
                if s.tail:
                    busy[SIDE1].append((tail_step, tail_at(o - 1, "product")))
                for kt in range(KT):
                    if kt < KT - 1:
                        scores(s.i, s.par, kt + 1)
                    elif s.more:
                        scores(s.i + 1, 1 - s.par, 0)
                    weighted(s.i, kt)
                    if kt == 0:
                        project_qk(s.i, 3)
                    if kt == 0 and s.pre:
                        transpose_xn(s.i)
                    if kt == 1 and s.pre:
                        project_v(s.i, 0)
                    if kt == 1 and s.tail:
                        transpose_y(o, SIDE0)
                    if kt == 2 and s.pre:
                        project_v(s.i, 1)
                    if 2 <= kt <= 4 and s.qk:
                        project_qk(s.i + 1, kt - 2)
                    if kt == 3 and s.tail:
                        feed_k(o, SIDE0)
                    if kt == 4 and s.tail:
                        feed_r(o, SIDE0)
                    if kt == 5 and s.tail:
                        feed_v(o, SIDE1)
                    if kt >= 5 and s.post:
                        project_out(n, kt - 5)

            def last_slot(n, a, o, par, more=True):
                if n is not None:
                    busy[SIDE0] = [(post_step, post_at(a, "bias"))]
                if o is not None:
                    busy[SIDE1] = [(tail_step, tail_at(o - 1, "product"))]
                    busy[LAST_K] = [(ff_step, ff_at(o - 1, "relu")), (c_out_done, SLOTS + 1)]
                    busy[LAST_R] = [(ff_step, ff_at(o - 1, "exp")), (c_out_done, SLOTS + 1)]
                    feed_k(o, LAST_K)
                    feed_r(o, LAST_R)
                if n is not None:
                    for part in range(2):
                        project_out(n, part, 1 - par)
                if a is not None:
                    busy[LAST_Y] = [(y_step, y_at(a - 1, 2)), (exp_done, exp_at(SLOTS - 1, KT - 1, 1))]
                    transpose_y(a, LAST_Y)
                if o is not None:
                    feed_v(o, SIDE1)
                if n is not None:
                    project_out(n, 2, 1 - par)

            walk(pe.Fori, first_tiles, slot, last_slot)


def kernel(**inputs):
    import numpy as np
    import concourse.bacc as bacc
    from concourse.bass_utils import run_bass_kernel_spmd as run

    f = {k.replace("L0_", ""): np.asarray(v) for k, v in inputs.items()}
    x = f["attn_x"]
    B, S, D = x.shape
    H, Dh, _ = f["attn_q_w"].shape
    pairs, chunks = H * Dh // P, D // P

    def chunked(w):
        return w.T.reshape(chunks, P, -1).transpose(1, 0, 2)

    def by_pair(w):
        return chunked(w.reshape(H * Dh, D)).reshape(P, chunks, pairs, P).transpose(2, 0, 1, 3)

    wqk = np.concatenate([by_pair(f["attn_q_w"]), by_pair(f["attn_k_w"])], axis=-1)
    bqk = np.stack([f["attn_q_b"].reshape(pairs, P).T, f["attn_k_b"].reshape(pairs, P).T], axis=1)
    laid = {
        "x": x.reshape(B * S, D),
        "wqk": np.concatenate([wqk, wqk[:1]]),
        "bqk": np.concatenate([bqk, bqk[:, :, :1]], axis=-1),
        "wv": chunked(f["attn_v_w"].reshape(H * Dh, D)),
        "vb": f["attn_v_b"].reshape(H * Dh),
        "wl": f["attn_l_w"].T.reshape(pairs, P, D).transpose(1, 0, 2).reshape(P, 2, -1),
        "lb": f["attn_l_b"].reshape(D),
        "ffn": np.stack([chunked(f[f"ffn_W_{n}"]).reshape(P, -1) for n in "rkv"], axis=1),
        "mu": np.stack([f[f"ffn_mu_{n}"].reshape(chunks, P).T for n in "rk"], axis=1),
    }
    laid = {k: np.ascontiguousarray(v) for k, v in laid.items()}
    nc = bacc.Bacc("TRN2", target_bir_lowering=False, num_devices=1)
    aps = {k: nc.dram_tensor(f"in_{k}", v.shape, F32, kind="ExternalInput").ap() for k, v in laid.items()}
    out = nc.dram_tensor("out", (B * S, D), F32, kind="ExternalOutput").ap()
    v_scr = nc.dram_tensor("v_scr", (B, pairs, P, S // P, P), F32, kind="Internal").ap()
    c_scr = nc.dram_tensor("c_scr", (B, S // P, P, pairs, P), F32, kind="Internal").ap()
    attention_ffn_block(nc, out=out, v_scr=v_scr, c_scr=c_scr, **aps)
    r = run(nc, [{f"in_{k}": v for k, v in laid.items()}], core_ids=[0])
    return r.results[0]["out"].reshape(B, S, D)
```
